# Optimizing a Trainium2 kernel written in Bass

```python
import numpy as np
import jax
import jax.numpy as jnp

def _softmax(x, axis=-1):
    return jax.nn.softmax(x, axis=axis)

def _gelu(x):
    return jax.nn.gelu(x, approximate=True)

def _silu(x):
    return jax.nn.silu(x)

def _sigmoid(x):
    return jax.nn.sigmoid(x)

def _layernorm(x, axis=-1, eps=1e-05):
    m = jnp.mean(x, axis=axis, keepdims=True)
    v = jnp.var(x, axis=axis, keepdims=True)
    return (x - m) / jnp.sqrt(v + eps)

def _scatter_add(tgt, idx, src, axis=0):
    return tgt.at[idx].add(src)

def _segment_sum(src, seg, n):
    return jax.ops.segment_sum(src, seg, n)
kernel_name = 'mk_vit_tower_d1_tok_img1024_r4_97afcf'

def setup_inputs(seed: int=0):
    np.random.seed(seed)
    _w = jnp.asarray

    def _rec_inputs():
        import jax
        import jax.numpy as jnp
        _rk = jax.random.key(seed)
        x = -0.000392918 + 0.999932 * jax.random.normal(jax.random.fold_in(_rk, 1), (16, 256, 256, 1), jnp.float32)
        return x
    x = _rec_inputs()

    def _L0_tok_setup():
        import jax, jax.numpy as jnp
        import numpy as np
        INV_SQRT2 = 0.7071067811865476
        LEVEL = 3

        def _split(x, axis):
            ax = axis % x.ndim
            sl0 = [slice(None)] * x.ndim
            sl0[ax] = slice(0, None, 2)
            sl1 = [slice(None)] * x.ndim
            sl1[ax] = slice(1, None, 2)
            x0, x1 = (x[tuple(sl0)], x[tuple(sl1)])
            return ((x0 + x1) * INV_SQRT2, (x0 - x1) * INV_SQRT2)

        def _merge(lo, hi, axis):
            ax = axis % lo.ndim
            e = (lo + hi) * INV_SQRT2
            o = (lo - hi) * INV_SQRT2
            s = jnp.stack([e, o], axis=ax + 1)
            shape = list(lo.shape)
            shape[ax] *= 2
            return s.reshape(shape)

        def _dwt2(x):
            lo, hi = _split(x, -1)
            a, h = _split(lo, -2)
            v, d = _split(hi, -2)
            return (a, h, v, d)

        def _idwt2(a, h, v, d):
            lo = _merge(a, h, -2)
            hi = _merge(v, d, -2)
            return _merge(lo, hi, -1)
        key = jax.random.key(seed)
        ks = jax.random.split(key, 8)
        B, H, W = (16, 256, 256)
        x = jax.random.normal(ks[0], (B, H, W, 1), dtype=jnp.float32)
        na = H // 8 * (W // 8)
        n2 = H // 4 * (W // 4)
        n1 = H // 2 * (W // 2)
        scale = 0.02
        Wa = jax.random.normal(ks[1], (na, 1), dtype=jnp.float32) * scale
        ba = jnp.zeros((1,), jnp.float32)
        Wd1 = jax.random.normal(ks[2], (3 * na, 3), dtype=jnp.float32) * scale
        bd1 = jnp.zeros((3,), jnp.float32)
        Wd2 = jax.random.normal(ks[3], (3 * n2, 3), dtype=jnp.float32) * scale
        bd2 = jnp.zeros((3,), jnp.float32)
        Wd3 = jax.random.normal(ks[4], (3 * n1, 3), dtype=jnp.float32) * scale
        bd3 = jnp.zeros((3,), jnp.float32)
        return {'x': x, 'Wa': Wa, 'ba': ba, 'Wd1': Wd1, 'bd1': bd1, 'Wd2': Wd2, 'bd2': bd2, 'Wd3': Wd3, 'bd3': bd3}
    _L0_tok_all = _L0_tok_setup()
    _L0_tok_in = {k: v for k, v in _L0_tok_all.items() if k in ('Wa', 'ba', 'Wd1', 'bd1', 'Wd2', 'bd2', 'Wd3', 'bd3')}
    del _L0_tok_all

    def _L0_attn_setup():
        import jax, jax.numpy as jnp
        import numpy as np
        HEAD_NUM = 16
        NEG_BIG = 1000000.0
        key = jax.random.key(seed)
        ks = jax.random.split(key, 5)
        E = 256
        B, S = (1, 1024)
        x = jax.random.normal(ks[0], (B, S, E), dtype=jnp.float32)
        W1 = jax.random.normal(ks[1], (E, 3 * E), dtype=jnp.float32) * (1.0 / np.sqrt(E))
        b1 = jax.random.normal(ks[2], (3 * E,), dtype=jnp.float32) * 0.02
        Wp = jax.random.normal(ks[3], (E, E), dtype=jnp.float32) * (1.0 / np.sqrt(E))
        bp = jax.random.normal(ks[4], (E,), dtype=jnp.float32) * 0.02
        return {'x': x, 'W1': W1, 'b1': b1, 'Wp': Wp, 'bp': bp}
    _L0_attn_all = _L0_attn_setup()
    _L0_attn_in = {k: v for k, v in _L0_attn_all.items() if k in ('W1', 'b1', 'Wp', 'bp')}
    del _L0_attn_all

    def _L0_ffn_setup():
        import jax, jax.numpy as jnp
        import numpy as np
        B, S, H = (8, 1024, 256)
        NAV = 128
        E = 8
        F = 2 * H
        key = jax.random.key(seed)
        ks = jax.random.split(key, 12)

        def w(k, shape, fan_in):
            return jax.random.normal(k, shape, dtype=jnp.float32) / np.sqrt(fan_in)
        return {'hidden_states': jax.random.normal(ks[0], (B, S, H), dtype=jnp.float32), 'Wp1': w(ks[1], (H, NAV), H), 'bp1': jnp.zeros((NAV,), jnp.float32), 'Wp2': w(ks[2], (NAV, E), NAV), 'bp2': jnp.zeros((E,), jnp.float32), 'W1': w(ks[3], (E, H, F), H), 'b1': jnp.zeros((E, F), jnp.float32), 'W2': w(ks[4], (E, F, H), F), 'b2': jnp.zeros((E, H), jnp.float32), 'Wo': w(ks[5], (H, H), H), 'bo': jnp.zeros((H,), jnp.float32)}
    _L0_ffn_all = _L0_ffn_setup()
    _L0_ffn_in = {k: v for k, v in _L0_ffn_all.items() if k in ('Wp1', 'bp1', 'Wp2', 'bp2', 'W1', 'b1', 'W2', 'b2', 'Wo', 'bo')}
    del _L0_ffn_all
    return {'x': x, 'L0_tok_Wa': _L0_tok_in['Wa'], 'L0_tok_ba': _L0_tok_in['ba'], 'L0_tok_Wd1': _L0_tok_in['Wd1'], 'L0_tok_bd1': _L0_tok_in['bd1'], 'L0_tok_Wd2': _L0_tok_in['Wd2'], 'L0_tok_bd2': _L0_tok_in['bd2'], 'L0_tok_Wd3': _L0_tok_in['Wd3'], 'L0_tok_bd3': _L0_tok_in['bd3'], 'L0_attn_W1': _L0_attn_in['W1'], 'L0_attn_b1': _L0_attn_in['b1'], 'L0_attn_Wp': _L0_attn_in['Wp'], 'L0_attn_bp': _L0_attn_in['bp'], 'L0_ffn_Wp1': _L0_ffn_in['Wp1'], 'L0_ffn_bp1': _L0_ffn_in['bp1'], 'L0_ffn_Wp2': _L0_ffn_in['Wp2'], 'L0_ffn_bp2': _L0_ffn_in['bp2'], 'L0_ffn_W1': _L0_ffn_in['W1'], 'L0_ffn_b1': _L0_ffn_in['b1'], 'L0_ffn_W2': _L0_ffn_in['W2'], 'L0_ffn_b2': _L0_ffn_in['b2'], 'L0_ffn_Wo': _L0_ffn_in['Wo'], 'L0_ffn_bo': _L0_ffn_in['bo']}

def reference(x, L0_tok_Wa, L0_tok_ba, L0_tok_Wd1, L0_tok_bd1, L0_tok_Wd2, L0_tok_bd2, L0_tok_Wd3, L0_tok_bd3, L0_attn_W1, L0_attn_b1, L0_attn_Wp, L0_attn_bp, L0_ffn_Wp1, L0_ffn_bp1, L0_ffn_Wp2, L0_ffn_bp2, L0_ffn_W1, L0_ffn_b1, L0_ffn_W2, L0_ffn_b2, L0_ffn_Wo, L0_ffn_bo):
    import jax
    import jax.numpy as jnp

    def _L0_tok_ref(x, Wa, ba, Wd1, bd1, Wd2, bd2, Wd3, bd3):
        import jax, jax.numpy as jnp
        import numpy as np
        INV_SQRT2 = 0.7071067811865476
        LEVEL = 3

        def _split(x, axis):
            ax = axis % x.ndim
            sl0 = [slice(None)] * x.ndim
            sl0[ax] = slice(0, None, 2)
            sl1 = [slice(None)] * x.ndim
            sl1[ax] = slice(1, None, 2)
            x0, x1 = (x[tuple(sl0)], x[tuple(sl1)])
            return ((x0 + x1) * INV_SQRT2, (x0 - x1) * INV_SQRT2)

        def _merge(lo, hi, axis):
            ax = axis % lo.ndim
            e = (lo + hi) * INV_SQRT2
            o = (lo - hi) * INV_SQRT2
            s = jnp.stack([e, o], axis=ax + 1)
            shape = list(lo.shape)
            shape[ax] *= 2
            return s.reshape(shape)

        def _dwt2(x):
            lo, hi = _split(x, -1)
            a, h = _split(lo, -2)
            v, d = _split(hi, -2)
            return (a, h, v, d)

        def _idwt2(a, h, v, d):
            lo = _merge(a, h, -2)
            hi = _merge(v, d, -2)
            return _merge(lo, hi, -1)
        img = x[..., 0]
        B = img.shape[0]
        details = []
        cur = img
        for _ in range(LEVEL):
            cur, h, v, d = _dwt2(cur)
            details.append((h, v, d))
        aw = jax.nn.sigmoid(cur.reshape(B, -1) @ Wa + ba)
        rec = cur * aw[:, :, None]
        det_params = [(Wd1, bd1), (Wd2, bd2), (Wd3, bd3)]
        for (h, v, d), (Wd, bd) in zip(reversed(details), det_params):
            flat = jnp.stack([h, v, d], axis=1).reshape(B, -1)
            w = jax.nn.softmax(flat @ Wd + bd, axis=-1)
            rec = _idwt2(rec, h * w[:, 0, None, None], v * w[:, 1, None, None], d * w[:, 2, None, None])
        return rec

    def _L0_attn_ref(x, W1, b1, Wp, bp):
        import jax, jax.numpy as jnp
        import numpy as np
        HEAD_NUM = 16
        NEG_BIG = 1000000.0
        B, S, E = x.shape
        H = HEAD_NUM
        d = E // H
        dk = jnp.asarray(d, x.dtype) ** 0.5
        h = x @ W1 + b1
        h = jnp.swapaxes(h.reshape(B, S, H, 3 * d), 1, 2)
        q, k, v = (h[..., :d], h[..., d:2 * d], h[..., 2 * d:])
        w = jnp.einsum('bhqd,bhkd->bhqk', q, k) / dk
        mask = jnp.tril(jnp.ones((S, S), dtype=x.dtype))
        w = jax.nn.softmax(w * mask - (1.0 - mask) * NEG_BIG, axis=-1)
        a = jnp.einsum('bhqk,bhkd->bhqd', w, v)
        a = jnp.swapaxes(a, 1, 2).reshape(B, S, E)
        return a @ Wp + bp

    def _L0_ffn_ref(hidden_states, Wp1, bp1, Wp2, bp2, W1, b1, W2, b2, Wo, bo):
        import jax, jax.numpy as jnp
        import numpy as np
        B, S, H = (8, 1024, 256)
        NAV = 128
        E = 8
        F = 2 * H
        last = hidden_states[:, -1, :]
        logits = jax.nn.gelu(last @ Wp1 + bp1, approximate=False) @ Wp2 + bp2
        action_probs = jax.nn.softmax(logits, axis=-1)
        sel = jnp.argmax(action_probs, axis=-1)
        w1 = W1[sel]
        w2 = W2[sel]
        h = jax.nn.gelu(jnp.einsum('bsh,bhf->bsf', hidden_states, w1) + b1[sel][:, None, :], approximate=False)
        reasoned = jnp.einsum('bsf,bfh->bsh', h, w2) + b2[sel][:, None, :]
        out = reasoned @ Wo + bo
        return hidden_states + 0.3 * out
    h = _L0_tok_ref(x, L0_tok_Wa, L0_tok_ba, L0_tok_Wd1, L0_tok_bd1, L0_tok_Wd2, L0_tok_bd2, L0_tok_Wd3, L0_tok_bd3)
    h = h + _L0_attn_ref(_layernorm(h, axis=-1), L0_attn_W1, L0_attn_b1, L0_attn_Wp, L0_attn_bp)
    h = h + _L0_ffn_ref(_layernorm(h, axis=-1), L0_ffn_Wp1, L0_ffn_bp1, L0_ffn_Wp2, L0_ffn_bp2, L0_ffn_W1, L0_ffn_b1, L0_ffn_W2, L0_ffn_b2, L0_ffn_Wo, L0_ffn_bo)
    return h

_drawn_inputs = setup_inputs


def setup_inputs(seed=0):
    import zlib

    import numpy as np

    out = dict(_drawn_inputs(seed))
    spreads = {'L0_tok_bd1': (0.0, 0.519),
     'L0_tok_bd2': (0.0, 0.71),
     'L0_tok_bd3': (0.0, 0.8),
     'L0_ffn_bp1': (0.0, 0.1),
     'L0_ffn_bp2': (0.0, 0.1),
     'L0_ffn_b1': (0.0, 0.624),
     'L0_ffn_b2': (0.0, 0.413),
     'L0_ffn_bo': (0.0, 0.408)}
    factors = {}
    for name, (base, spread) in spreads.items():
        noise = np.random.default_rng([zlib.crc32(name.encode()), seed]).standard_normal(out[name].shape)
        drawn = base * np.exp(spread * noise) if base else spread * noise
        out[name] = jnp.asarray(drawn.astype(out[name].dtype))
    for name, factor in factors.items():
        out[name] = (out[name] * factor).astype(out[name].dtype)
    return out
```

```python
from contextlib import ExitStack

import numpy as np

import concourse.bass as bass
from concourse import mybir

F32 = mybir.dt.float32
BF16 = mybir.dt.bfloat16
U32 = mybir.dt.uint32
ALU = mybir.AluOpType
ACT = mybir.ActivationFunctionType
AX = mybir.AxisListType.X

P = 128
B, S, E = 16, 256, 256
H, D = 16, 16
NX, FF, NAV = 8, 512, 128
TT, CH, FT = S // P, E // P, FF // P
EPS = 1e-5
BLK = S // 8
IPT = P // BLK
TILES = B // IPT
UPI = 2
HU = H // UPI
UNITS = B * UPI
GH = 4
SLOTS = 6
KQ = SLOTS * D
KM = KQ + 3
RING = 4
BIG = -1.0e6
LVL = ((4, 128), (2, 64), (1, 32))
LW = [3 * r * c for r, c in LVL]
WD_OFF = [0, 3 * LW[0], 3 * (LW[0] + LW[1]), 3 * sum(LW)]
WD_W = 3 * sum(LW) + LVL[2][0] * LVL[2][1]
WX_W = CH * FF + FT * E + FT + CH


def tower(nc, x, wd, bd, w1, bqk, bv, wp, bp, wp1, bp1, wp2, bp2, wx, wo, bo, out):
    bounce = nc.dram_tensor("bounce", [RING, 2, 3, P, S], BF16).ap()
    with ExitStack() as ctx:
        def sb(name, shape, dt=F32):
            return ctx.enter_context(nc.sbuf_tensor(name, shape, dt))

        def sem(name):
            return ctx.enter_context(nc.semaphore(name))

        S1 = ctx.enter_context(nc.psum_tensor("S1", [P, 1536], F32))
        S2 = ctx.enter_context(nc.psum_tensor("S2", [P, 1536], F32))
        PO = ctx.enter_context(nc.psum_tensor("PO", [P, 512], F32))
        PM = ctx.enter_context(nc.psum_tensor("PM", [P, 512], F32))

        hN = sb("hN", [P, B * TT, E])
        ident = sb("ident", [P, P])
        identb = sb("identb", [P, P], BF16)
        maskb = sb("maskb", [P, P], BF16)
        blkones = sb("blkones", [P, P])
        half = sb("half", [P, 2])
        stat = sb("stat", [P, 2, TT, 6])
        mv = sb("mv", [P, 2, TT, 2])
        ve = sb("ve", [P, 2, TT])
        rstd = sb("rstd", [P, 2, TT])
        xn = sb("xn", [P, 2, TT, E])
        xT = sb("xT", [P, 2, CH, S])
        arena = sb("arena", [P, 15700])
        cur = [0]

        def carve(n):
            a = arena[:, cur[0]:cur[0] + n]
            cur[0] += n
            return a

        X = carve(8 * E)
        LO = [carve(2 * r * c) for r, c in LVL]
        HI = [carve(2 * r * c) for r, c in LVL]
        DT = [carve(n) for n in LW]
        AA = [carve(r * c) for r, c in LVL]
        REC = [X, AA[0], AA[1]]
        RX = carve(8 * E)
        WD = carve(WD_W)
        part = carve(10)
        z = carve(10)
        ez = carve(10)
        es = carve(10)
        zmax = carve(3)
        zsum = carve(4)
        zrec = carve(4)
        wg = carve(10)
        bdt = carve(10)
        wscale = carve(10)
        assert cur[0] <= 15700
        cur[0] = 0
        WX = [carve(WX_W) for _ in range(2)]
        gT = [carve(FT * S) for _ in range(2)]
        rT = [carve(CH * S) for _ in range(2)]
        fin = [carve(TT * E) for _ in range(2)]
        wo_sb = carve(CH * E)
        bo3 = carve(E)
        wp1_sb = carve(CH * NAV)
        wp2_sb = carve(NX)
        bp1_sb = carve(1)
        bp2_sb = carve(NX)
        lastr = carve(E)
        lstat = carve(6)
        lmv = carve(2)
        lve = carve(1)
        lrstd = carve(1)
        lastT = carve(CH * B)
        gact = carve(B)
        logit = carve(NX)
        top8 = carve(NX)
        assert cur[0] <= 15700
        idx8 = sb("idx8", [B, 8], U32)
        idxr = sb("idxr", [1, B], U32)

        w1_sb = sb("w1_sb", [P, CH, 3, E])
        wp_sb = sb("wp_sb", [P, UPI, E])
        bqk_sb = sb("bqk_sb", [P, UPI, 2])
        bv_sb = sb("bv_sb", [P, E])
        bp_sb = sb("bp_sb", [P, E])
        QF = sb("QF", [P, 2, 2, S])
        QR = sb("QR", [P, 2, 2, S])
        QB = sb("QB", [P, 2, 2, 3, S], BF16)
        QP = sb("QP", [P, RING, HU, S], BF16)
        KP = sb("KP", [P, RING, HU, S], BF16)
        Va = sb("Va", [P, 2, TT, H, D, 2])
        PT = sb("PT", [P, 2, 1536])
        OS = sb("OS", [P, 2, 2, S])
        AU = sb("AU", [P, 2, S])
        SC = sb("SC", [P, 2, S])
        AC = sb("AC", [P, RING, S])
        mx = sb("mx", [P, 2, TT * HU])
        mF = sb("mF", [TT * HU, 2, P])
        mR = sb("mR", [TT * HU, 2, P])
        mB = sb("mB", [TT * HU, 2, 3, P], BF16)

        s_cst = sem("s_cst")
        s_x = sem("s_x")
        s_wd = sem("s_wd")
        s_wts = sem("s_wts")
        s_xfree = sem("s_xfree")
        s_part = sem("s_part")
        s_zps = sem("s_zps")
        s_z = sem("s_z")
        s_ez = sem("s_ez")
        s_wg = sem("s_wg")
        s_gate = sem("s_gate")
        s_rec = sem("s_rec")
        s_h0 = sem("s_h0")
        s_stat = sem("s_stat")
        s_rstd = sem("s_rstd")
        s_xn = sem("s_xn")
        s_bp = sem("s_bp")
        s_tr = sem("s_tr")
        s_xt = sem("s_xt")
        s_d = sem("s_d")
        s_qa = sem("s_qa")
        s_hi = sem("s_hi")
        s_r1 = sem("s_r1")
        s_mid = sem("s_mid")
        s_lo = sem("s_lo")
        s_scr = sem("s_scr")
        s_qp = [sem(f"s_qp{r}") for r in range(RING)]
        s_p1 = sem("s_p1")
        s_mx = sem("s_mx")
        s_mt = sem("s_mt")
        s_mf = sem("s_mf")
        s_ms = sem("s_ms")
        s_mrow = sem("s_mrow")
        s_p2 = sem("s_p2")
        s_exp = sem("s_exp")
        s_sel = sem("s_sel")
        s_pv = sem("s_pv")
        s_os = sem("s_os")
        s_oc = [sem(f"s_oc{b}") for b in range(2)]
        s_ac = sem("s_ac")
        s_v = sem("s_v")
        s_va = sem("s_va")
        s_wp = sem("s_wp")
        s_h2 = sem("s_h2")
        s_turn = sem("s_turn")
        sp_turn = sem("sp_turn")
        f_w = sem("f_w")
        f_last = sem("f_last")
        f_lst = sem("f_lst")
        f_lrs = sem("f_lrs")
        f_ln = sem("f_ln")
        f_lt = sem("f_lt")
        f_lte = sem("f_lte")
        f_ga = sem("f_ga")
        f_gae = sem("f_gae")
        f_lg = sem("f_lg")
        f_idx = sem("f_idx")
        f_idr = sem("f_idr")
        f_wx = [sem(f"f_wx{b}") for b in range(2)]
        f_stat = sem("f_stat")
        f_rstd = sem("f_rstd")
        f_xn = sem("f_xn")
        f_base = sem("f_base")
        f_tr = sem("f_tr")
        f_xt = sem("f_xt")
        f_u = sem("f_u")
        f_g = sem("f_g")
        f_d = sem("f_d")
        f_r = sem("f_r")
        f_y = sem("f_y")
        f_fin = sem("f_fin")
        f_out = [sem(f"f_out{b}") for b in range(2)]

        def need(eng, s, v):
            if not isinstance(v, int) or v > 0:
                eng.wait_ge(s, v)

        def h_row(n, tt):
            return hN[:, bass.ds(n * TT + tt, 1), :].rearrange("p o e -> p (o e)")

        def bcast(ap, shape):
            return ap.to_broadcast(shape)

        FIRST, LAST = -2 * UPI, UNITS + 1
        LOOP0, LOOPS = 4, 5

        def slots(eng, body):
            for u in range(FIRST, LOOP0):
                body(u, u // 2, u, 0)
            with eng.Fori(0, LOOPS) as it:
                for k in range(4):
                    body(it * 4 + (LOOP0 + k), it * 2 + (LOOP0 + k) // 2, k, it + LOOP0 // RING)
            for u in range(LOOP0 + 4 * LOOPS, LAST + 1):
                body(u, u // 2, u, 0)

        def images(eng, body, count):
            for n in range(2):
                body(n, n, 0)
            with eng.Fori(1, count // 2) as it:
                for b in range(2):
                    body(it * 2 + b, b, it)
            for n in range(count // 2 * 2, count):
                body(n, n % 2, n // 2)

        def unit_ok(u):
            return not isinstance(u, int) or 0 <= u < UNITS

        def image_ok(n):
            return not isinstance(n, int) or 0 <= n < B

        def y_ps(b):
            return (S1 if b == 0 else S2)[:, 1024:1536]

        block = ctx.enter_context(nc.Block())

        @block.gpsimd
        def _(pool):
            pool.memset(ident[:, :], 0.0).then_inc(s_cst, 1)
            pool.memset(identb[:, :], 0.0).then_inc(s_cst, 1)
            pool.memset(maskb[:, :], 0.0).then_inc(s_cst, 1)
            pool.memset(blkones[:, :], 0.0).then_inc(s_cst, 1)
            pool.memset(half[:, :], -0.5).then_inc(s_cst, 1)
            pool.wait_ge(s_cst, 5)
            pool.memset(KP[96:P, :, :, :], 1.0).then_inc(s_cst, 1)
            pool.wait_ge(s_cst, 6)
            pool.memset(Va[:, :, :, :, :, 1], 1.0).then_inc(s_cst, 1)
            for l in range(3):
                pool.memset(wscale[:, 3 * l:3 * l + 3], 0.25 ** (l + 1)).then_inc(s_cst, 1)
            pool.memset(wscale[:, 9:10], 0.25 ** 3).then_inc(s_cst, 1)
            pool.wait_ge(s_cst, 11)
            for m in (ident, identb):
                pool.affine_select(out=m[:, :], in_=m[:, :], compare_op=ALU.not_equal, fill=1.0, base=0,
                                   pattern=[[-1, P]], channel_multiplier=1).then_inc(s_cst, 1)
            pool.affine_select(out=maskb[:, :], in_=maskb[:, :], compare_op=ALU.is_ge, fill=BIG, base=0,
                               pattern=[[-1, P]], channel_multiplier=1).then_inc(s_cst, 1)
            for i in range(IPT):
                pool.wait_ge(s_cst, 14 + i)
                pool.memset(blkones[BLK * i:BLK * i + BLK, BLK * i:BLK * i + BLK], 1.0).then_inc(s_cst, 1)

            def slot(u, n, k, lap):
                w, odd = u + 3, k % 2
                if not odd and image_ok(n + 2):
                    need(pool, s_xn, n + 3)
                    for tt in range(TT):
                        a = h_row(n + 2, tt)
                        pool.tensor_tensor(a, a, bp_sb[:, :], ALU.add).then_inc(s_bp, 1)
                if unit_ok(w):
                    b = (k + 3) % 2
                    need(pool, s_hi, w + 1)
                    need(pool, s_lo, w - 1)
                    pool.tensor_tensor(QR[:, b, :, :], QF[:, b, :, :], QB[:, b, :, 0, :],
                                       ALU.subtract).then_inc(s_r1, 1)
                if unit_ok(u):
                    select(u, 0)
                if unit_ok(w):
                    b = (k + 3) % 2
                    need(pool, s_mid, w + 1)
                    pool.tensor_tensor(QB[:, b, :, 2, :], QR[:, b, :, :], QB[:, b, :, 1, :],
                                       ALU.subtract).then_inc(s_lo, 1)
                if unit_ok(u):
                    select(u, 1)
                if odd and image_ok(n + 3):
                    b = (k // 2 + 3) % 2
                    need(pool, s_stat, n + 4)
                    pool.tensor_tensor(rstd[:, b, :], ve[:, b, :], half[:, :], ALU.pow).then_inc(s_rstd, 1)

            def select(u, g):
                need(pool, s_exp, u * 2 + (g + 1))
                pool.sem_inc(s_turn, 1)
                pt = PT[:, g, :]
                for v in (pt[:, 0:1024].rearrange("p (h q) -> p h q", h=GH)[:, :, 0:P],
                          pt[:, 1024:1536].rearrange("p (h q) -> p h q", h=GH)):
                    pool.affine_select(out=v, in_=v, compare_op=ALU.is_ge, fill=0.0, base=0,
                                       pattern=[[0, GH], [1, P]], channel_multiplier=-1).then_inc(s_sel, 1)

            pool.wait_ge(s_cst, 18)
            pool.wait_ge(s_wts, 16 * 5)
            for n in range(1):
                pool.wait_ge(s_stat, n + 1)
                pool.tensor_tensor(rstd[:, n % 2, :], ve[:, n % 2, :], half[:, :], ALU.pow).then_inc(s_rstd, 1)
            slots(pool, slot)

            pool.wait_ge(f_lst, 1)
            pool.tensor_tensor(lrstd[0:B, :], lve[0:B, :], half[0:B, 0:1], ALU.pow).then_inc(f_lrs, 1)

            def ffn(n, b, m):
                need(pool, f_stat, n + 1)
                pool.tensor_tensor(rstd[:, b, :], ve[:, b, :], half[:, :], ALU.pow).then_inc(f_rstd, 1)
                need(pool, f_xn, n + 1)
                for tt in range(TT):
                    a = h_row(n, tt)
                    pool.tensor_tensor(a, a, xn[:, b, tt, :], ALU.add).then_inc(f_base, 1)

            images(pool, ffn, B)

        @block.sync
        def _(sp):
            def need_sp(s, v):
                need(sp, s, v)
                if not isinstance(v, int):
                    sp.sem_inc(sp_turn, 1)

            sp.dma_start(X, x[0]).then_inc(s_x, 16)
            for i in range(IPT):
                sp.dma_start(WD[BLK * i:BLK * i + BLK, :], wd).then_inc(s_wd, 16)
            sp.dma_start(bdt, bcast(bd, [P, 10])).then_inc(s_wd, 16)
            sp.dma_start(w1_sb[:, :, :, :], w1).then_inc(s_wts, 16)
            sp.dma_start(wp_sb[:, :, :], wp).then_inc(s_wts, 16)
            sp.dma_start(bqk_sb[:, :, :], bqk).then_inc(s_wts, 16)
            sp.dma_start(bv_sb[:, :], bcast(bv, [P, E])).then_inc(s_wts, 16)
            sp.dma_start(bp_sb[:, :], bcast(bp, [P, E])).then_inc(s_wts, 16)

            def rows_out(t):
                need_sp(s_rec, t + 1)
                for i in range(IPT):
                    for tt in range(TT):
                        p0 = BLK * i + BLK // TT * tt
                        sp.dma_start(h_row(t * IPT + i, tt),
                                     RX[p0:p0 + BLK // TT, :].rearrange("p (r e) -> p r e", r=8)).then_inc(s_h0, 16)

            with sp.Fori(0, TILES - 1) as t:
                need_sp(s_xfree, t + 1)
                sp.dma_start(X, x[bass.ds(t + 1, 1)].rearrange("o p c -> (o p) c")).then_inc(s_x, 16)
                rows_out(t)
            rows_out(TILES - 1)

            def slot(u, n, k, lap):
                v, w = u + 1, u + 3
                if unit_ok(u - 1):
                    b = (k - 1) % 2
                    need_sp(s_os, u)
                    need_sp(s_ac, u - 2)
                    for c, dst in ((0, AU), (1, SC)):
                        sp.dma_start(dst[:, b, :], OS[c:P:2, b, :, :]).then_inc(s_oc[b], 16)
                if unit_ok(w):
                    r = (k + 3) % RING
                    need_sp(s_lo, w + 1)
                    need_sp(s_qp[r], (lap + (k + 3) // RING) * 96)
                    sp.dma_start(bounce[r].rearrange("o s p t -> p (o s) t"),
                                 QB[:, (k + 3) % 2, :, :, :].rearrange("p o s t -> p (o s) t")).then_inc(s_scr, 16)
                if unit_ok(v):
                    need_sp(s_ms, v + 1)
                    for s in range(3):
                        sp.dma_start(QP[KQ + s:KQ + s + 1, (k + 1) % RING, :, :].rearrange(
                            "p h (t q) -> p (h t) q", t=TT), mB[:, (k + 1) % 2, s, :]).then_inc(s_mrow, 16)
                if unit_ok(w):
                    need_sp(s_scr, (w + 1) * 16)
                    need_sp(s_p2, (w - 3) * 2)
                    for o, dst, plan in ((0, QP, ((0, 0, 3, 3), (3, 0, 2, 2), (5, 0, 1, 1))),
                                         (1, KP, ((0, 0, 1, 3), (3, 1, 1, 2), (5, 2, 1, 1)))):
                        for at, part0, parts, count in plan:
                            src = bounce[r, o, part0:part0 + parts].rearrange("s (d h) t -> (s d) (h t)", h=HU)
                            if parts < count:
                                src = bounce[r, o, part0:part0 + 1].rearrange(
                                    "s (d h) t -> s d (h t)", h=HU).to_broadcast([count, D, HU * S])
                            sp.dma_start(dst[at * D:(at + count) * D, r, :, :], src).then_inc(s_qp[r], 16)

            slots(sp, slot)

            sp.wait_ge(s_h0, 16 * B * TT)
            sp.dma_start(wo_sb, wo).then_inc(f_w, 16)
            sp.dma_start(bo3, bcast(bo, [P, E])).then_inc(f_w, 16)
            sp.dma_start(wp1_sb, wp1).then_inc(f_w, 16)
            sp.dma_start(wp2_sb, wp2).then_inc(f_w, 16)
            sp.dma_start(bp1_sb, bp1).then_inc(f_w, 16)
            sp.dma_start(bp2_sb[0:B, :], bcast(bp2, [B, NX])).then_inc(f_w, 16)
            sp.wait_ge(s_h2, B)
            sp.dma_start(lastr[0:B, :], hN[P - 1:P, 1:B * TT:TT, :]).then_inc(f_last, 16)
            sp.wait_ge(f_idx, 1)
            sp.dma_start(idxr[:, :], idx8[:, 0:1]).then_inc(f_idr, 16)
            sp.wait_ge(f_idr, 16)

            def load_expert(n, b):
                need_sp(f_d, n - 1)
                e = sp.value_load(idxr[0:1, bass.ds(n, 1)], min_val=0, max_val=NX - 1)
                sp.dma_start(WX[b], wx[bass.ds(e, 1)].rearrange("o p c -> (o p) c")).then_inc(f_wx[b], 16)

            def store(n, b):
                need_sp(f_fin, (n + 1) * TT)
                sp.dma_start(out[bass.ds(n, 1)].rearrange("o (t p) e -> p (o t) e", p=P),
                             fin[b].rearrange("p (t e) -> p t e", t=TT)).then_inc(f_out[b], 16)

            def ffn(n, b, m):
                load_expert(n + 1, 1 - b)
                store(n, b)

            load_expert(0, 0)
            images(sp, ffn, B - 1)
            store(B - 1, 1)
            for b in range(2):
                sp.wait_ge(f_out[b], 16 * (B // 2))

        @block.scalar
        def _(act):
            dt3 = [DT[l].rearrange("p (k n) -> p k n", k=3) for l in range(3)]
            with act.Fori(0, TILES) as t:
                act.wait_ge(s_z, t + 1)
                nc.scalar.activation(ez, z, ACT.Exp).then_inc(s_ez, 1)
                act.wait_ge(s_wg, t + 1)
                nc.scalar.activation(AA[2], AA[2], ACT.Copy, scale=wg[:, 9:10]).then_inc(s_gate, 1)
                for l in (2, 1, 0):
                    for c in range(3):
                        nc.scalar.activation(dt3[l][:, c, :], dt3[l][:, c, :], ACT.Copy,
                                             scale=wg[:, 3 * l + c:3 * l + c + 1]).then_inc(s_gate, 1)

            def slot(u, n, k, lap):
                w, odd = u + 3, k % 2
                if unit_ok(w):
                    need(act, s_d, w + 1)
                    need(act, s_lo, w - 1)
                    b = (k + 3) % 2
                    for o in range(2):
                        ins = nc.scalar.activation(QF[:, b, o, :], PM[:, o * S:(o + 1) * S], ACT.Identity,
                                                   bias=bqk_sb[:, b, o:o + 1])
                    act.drain()
                    act.sem_inc(s_qa, 1)
                for g in range(2):
                    if unit_ok(u):
                        need(act, s_p2, u * 2 + (g + 1))
                        need(act, s_pv, u * 2 + (g - 1))
                        nc.scalar.activation(PT[:, g, :], S2[:, :], ACT.Exp, scale=float(D) ** -0.5).then_inc(s_exp, 1)
                if not odd and image_ok(n + 2):
                    need(act, s_tr, n + 3)
                    need(act, s_v, n + 1)
                    need(act, s_d, u + 2)
                    nc.scalar.copy(xT[:, (k // 2) % 2, :, :].rearrange("p c t -> p (c t)"), PM[:, :]).then_inc(s_xt, 1)
                if unit_ok(u):
                    need(act, s_pv, u * 2 + 2)
                    need(act, s_oc[k % 2], n * 32)
                    nc.scalar.copy(OS[:, k % 2, :, :].rearrange("p g t -> p (g t)"), PO[:, :]).then_inc(s_os, 1)

            slots(act, slot)

            act.wait_ge(f_ga, 1)
            act.wait_ge(f_w, 16 * 6)
            nc.scalar.activation(gact, PM[:, 0:B], ACT.Gelu, bias=bp1_sb).then_inc(f_gae, 1)

            def ffn(n, b, m):
                for j in range(2):
                    need(act, f_u, n * 2 + (j + 1))
                    if j == 0:
                        need(act, f_d, n - 1)
                    act.wait_ge(f_wx[b], (m + 1) * 16)
                    for c in range(2):
                        f = 2 * j + c
                        src = (S1 if b == 0 else S2)[:, f * S:(f + 1) * S]
                        nc.scalar.activation(gT[b][:, f * S:(f + 1) * S], src, ACT.Gelu,
                                             bias=WX[b][:, CH * FF + FT * E + f:CH * FF + FT * E + f + 1]).then_inc(f_g, 1)

            images(act, ffn, B)

        @block.vector
        def _(dve):
            tt_ = dve.tensor_tensor

            def analysis(src, l):
                r, c = LVL[l]
                s = src.rearrange("p (r c) -> p r c", r=2 * r)
                lo = LO[l].rearrange("p (r c) -> p r c", r=2 * r)
                hi = HI[l].rearrange("p (r c) -> p r c", r=2 * r)
                d = DT[l].rearrange("p (k r c) -> p k r c", k=3, r=r)
                a = AA[l].rearrange("p (r c) -> p r c", r=r)
                tt_(lo, s[:, :, 0::2], s[:, :, 1::2], ALU.add)
                ins = tt_(hi, s[:, :, 0::2], s[:, :, 1::2], ALU.subtract)
                dve.drain()
                tt_(a, lo[:, 0::2, :], lo[:, 1::2, :], ALU.add)
                tt_(d[:, 0], lo[:, 0::2, :], lo[:, 1::2, :], ALU.subtract)
                tt_(d[:, 1], hi[:, 0::2, :], hi[:, 1::2, :], ALU.add)
                tt_(d[:, 2], hi[:, 0::2, :], hi[:, 1::2, :], ALU.subtract)
                dve.drain()
                return ins

            def synthesis(dst, l):
                r, c = LVL[l]
                s = dst.rearrange("p (r c) -> p r c", r=2 * r)
                lo = LO[l].rearrange("p (r c) -> p r c", r=2 * r)
                hi = HI[l].rearrange("p (r c) -> p r c", r=2 * r)
                d = DT[l].rearrange("p (k r c) -> p k r c", k=3, r=r)
                a = AA[l].rearrange("p (r c) -> p r c", r=r)
                tt_(lo[:, 0::2, :], a, d[:, 0], ALU.add)
                tt_(lo[:, 1::2, :], a, d[:, 0], ALU.subtract)
                tt_(hi[:, 0::2, :], d[:, 1], d[:, 2], ALU.add)
                tt_(hi[:, 1::2, :], d[:, 1], d[:, 2], ALU.subtract)
                dve.drain()
                tt_(s[:, :, 0::2], lo, hi, ALU.add)
                return tt_(s[:, :, 1::2], lo, hi, ALU.subtract)

            dve.wait_ge(s_cst, 18)
            dve.wait_ge(s_wd, 16 * (IPT + 1))
            with dve.Fori(0, TILES) as t:
                dve.wait_ge(s_x, (t + 1) * 16)
                analysis(X, 0)
                dve.sem_inc(s_xfree, 1)
                analysis(AA[0], 1)
                analysis(AA[1], 2)
                need(dve, s_h0, t * (16 * IPT * TT))
                for l in range(3):
                    for j in range(3):
                        w0 = WD_OFF[l] + j * LW[l]
                        dve.tensor_tensor_reduce(RX[:, 0:LW[l]], DT[l], WD[:, w0:w0 + LW[l]], 0.5 ** (l + 1), 0.0,
                                                 ALU.mult, ALU.add, part[:, 3 * l + j:3 * l + j + 1])
                        dve.drain()
                na = LVL[2][0] * LVL[2][1]
                dve.tensor_tensor_reduce(RX[:, 0:na], AA[2], WD[:, WD_OFF[3]:WD_OFF[3] + na], 0.125, 0.0,
                                         ALU.mult, ALU.add, part[:, 9:10]).then_inc(s_part, 1)
                dve.wait_ge(s_zps, t + 1)
                tt_(z, PM[:, 0:10], bdt, ALU.add)
                dve.drain()
                z3 = z[:, 0:9].rearrange("p (l c) -> p l c", l=3)
                dve.tensor_reduce(zmax, z3, AX, ALU.max)
                dve.tensor_scalar(z[:, 9:10], z[:, 9:10], -1.0, None, ALU.mult)
                dve.drain()
                tt_(z3, z3, zmax.rearrange("p (l o) -> p l o", o=1).to_broadcast([P, 3, 3]),
                    ALU.subtract).then_inc(s_z, 1)
                dve.wait_ge(s_ez, t + 1)
                dve.tensor_reduce(zsum[:, 0:3], ez[:, 0:9].rearrange("p (l c) -> p l c", l=3), AX, ALU.add)
                dve.tensor_scalar(zsum[:, 3:4], ez[:, 9:10], 1.0, None, ALU.add)
                tt_(es[:, 0:9], ez[:, 0:9], wscale[:, 0:9], ALU.mult)
                dve.drain()
                dve.reciprocal(zrec, zsum)
                dve.drain()
                tt_(wg[:, 0:9].rearrange("p (l c) -> p l c", l=3), es[:, 0:9].rearrange("p (l c) -> p l c", l=3),
                    zrec[:, 0:3].rearrange("p (l o) -> p l o", o=1).to_broadcast([P, 3, 3]), ALU.mult)
                tt_(wg[:, 9:10], zrec[:, 3:4], wscale[:, 9:10], ALU.mult)
                dve.drain()
                dve.sem_inc(s_wg, 1)
                for l, gated in ((2, 4), (1, 7), (0, 10)):
                    dve.wait_ge(s_gate, t * 10 + gated)
                    ins = synthesis(RX if l == 0 else AA[l - 1], l)
                    if l:
                        dve.drain()
                ins.then_inc(s_rec, 1)
                dve.drain()

            def ln_stat(n, b, done):
                for tt in range(TT):
                    dve.bn_stats(stat[:, b, tt, :], h_row(n, tt))
                dve.drain()
                for tt in range(TT):
                    dve.bn_aggr(mv[:, b, tt, :], stat[:, b, tt, :])
                dve.drain()
                dve.tensor_scalar(ve[:, b, :], mv[:, b, :, 1], EPS, None, ALU.add).then_inc(done, 1)

            def ln_apply(n, b, rs, free, freed, done):
                need(dve, rs, n + 1)
                need(dve, free, freed)
                for tt in range(TT):
                    ins = dve.tensor_scalar(xn[:, b, tt, :], h_row(n, tt), mv[:, b, tt, 0:1], rstd[:, b, tt:tt + 1],
                                            ALU.subtract, ALU.mult)
                dve.drain()
                dve.sem_inc(done, 1)

            def slot(u, n, k, lap):
                v, w, odd = u + 1, u + 3, k % 2
                if not odd and image_ok(n + 2):
                    ln_apply(n + 2, (k // 2) % 2, s_rstd, s_tr, n + 1, s_xn)
                if unit_ok(v):
                    row_max(v, k + 1, 0)
                if unit_ok(w):
                    b = (k + 3) % 2
                    need(dve, s_qa, w + 1)
                    need(dve, s_scr, (w - 1) * 16)
                    dve.tensor_copy(QB[:, b, :, 0, :], QF[:, b, :, :]).then_inc(s_hi, 1)
                if unit_ok(u - 1):
                    b = (k - 1) % 2
                    need(dve, s_oc[b], (n + odd) * 32)
                    dve.reciprocal(SC[:, b, :], SC[:, b, :])
                    dve.drain()
                    m = n - 2 if odd else n - 3
                    need(dve, s_wp, m + 1)
                    tt_(AC[:, (k - 1) % RING, :], AU[:, b, :], SC[:, b, :], ALU.mult).then_inc(s_ac, 1)
                if unit_ok(v):
                    row_max(v, k + 1, 1)
                if unit_ok(w):
                    b = (k + 3) % 2
                    need(dve, s_r1, w + 1)
                    dve.tensor_copy(QB[:, b, :, 1, :], QR[:, b, :, :]).then_inc(s_mid, 1)
                if not odd and image_ok(n + 1):
                    need(dve, s_v, n + 2)
                    need(dve, s_pv, n * 4)
                    tt_(Va[:, (k // 2 + 1) % 2, :, :, :, 0], PM[:, :].rearrange("p (t h d) -> p t h d", t=TT, h=H),
                        bv_sb[:, :].rearrange("p (o h d) -> p o h d", o=1, h=H).to_broadcast([P, TT, H, D]),
                        ALU.add).then_inc(s_va, 1)
                if odd and image_ok(n - 1):
                    need(dve, s_wp, n)
                    need(dve, s_bp, n * TT)
                    a = hN[:, bass.ds((n - 1) * TT, TT), :]
                    tt_(a, a, PM[:, :].rearrange("p (t e) -> p t e", t=TT), ALU.add).then_inc(s_h2, 1)
                if unit_ok(v):
                    b = (k + 1) % 2
                    need(dve, s_mt, v + 1)
                    need(dve, s_mrow, (v - 1) * 48)
                    dve.tensor_scalar(mF[:, b, :], PM[0:TT * HU, 0:P], -1.0, None, ALU.mult).then_inc(s_mf, 1)
                    dve.drain()
                    dve.tensor_copy(mB[:, b, 0, :], mF[:, b, :])
                    dve.drain()
                    tt_(mR[:, b, :], mF[:, b, :], mB[:, b, 0, :], ALU.subtract)
                    dve.drain()
                    dve.tensor_copy(mB[:, b, 1, :], mR[:, b, :])
                    dve.drain()
                    tt_(mB[:, b, 2, :], mR[:, b, :], mB[:, b, 1, :], ALU.subtract).then_inc(s_ms, 1)
                if odd and image_ok(n + 3):
                    if not isinstance(n, int) or n + 3 >= 0:
                        dve.wait_ge(s_h0, 16 * B * TT)
                        ln_stat(n + 3, (k // 2 + 3) % 2, s_stat)

            def row_max(v, kv, g):
                b = kv % 2
                need(dve, s_p1, v * 2 + (g + 1))
                need(dve, s_mt, v - 1)
                m = mx[:, b, :].rearrange("p (h t) -> p h t", t=TT)[:, GH * g:GH * (g + 1), :]
                dve.tensor_reduce(m[:, :, 1],
                                  S1[:, 0:1024].rearrange("p (h q) -> p h q", h=GH), AX, ALU.max).then_inc(s_mx, 1)
                dve.tensor_reduce(m[:, :, 0],
                                  S1[:, 1024:1536].rearrange("p (h q) -> p h q", h=GH), AX, ALU.max).then_inc(s_mx, 1)

            dve.wait_ge(s_wts, 16 * 5)
            dve.wait_ge(s_h0, 16 * B * TT)
            ln_stat(0, 0, s_stat)
            slots(dve, slot)

            dve.wait_ge(f_last, 16)
            dve.wait_ge(f_w, 16 * 6)
            dve.bn_stats(lstat[0:B, :], lastr[0:B, :])
            dve.drain()
            dve.bn_aggr(lmv[0:B, :], lstat[0:B, :])
            dve.drain()
            dve.tensor_scalar(lve[0:B, :], lmv[0:B, 1:2], EPS, None, ALU.add).then_inc(f_lst, 1)
            dve.tensor_scalar(bo3, bo3, 0.3, None, ALU.mult)
            dve.wait_ge(f_lrs, 1)
            dve.tensor_scalar(lastr[0:B, :], lastr[0:B, :], lmv[0:B, 0:1], lrstd[0:B, :], ALU.subtract,
                              ALU.mult).then_inc(f_ln, 1)
            dve.wait_ge(f_lt, 1)
            dve.tensor_copy(lastT.rearrange("p (c n) -> p c n", c=CH),
                            PM[:, 0:CH * B].rearrange("p (c n) -> p c n", c=CH)).then_inc(f_lte, 1)
            dve.wait_ge(f_lg, 1)
            tt_(logit[0:B, :], PM[0:B, 0:NX], bp2_sb[0:B, :], ALU.add)
            dve.drain()
            dve.max(top8[0:B, :], logit[0:B, :])
            dve.drain()
            dve.max_index(idx8[:, :], top8[0:B, :], logit[0:B, :]).then_inc(f_idx, 1)

            def ffn_in(n, b):
                ln_stat(n, b, f_stat)
                need(dve, f_base, (n - 1) * TT)
                ln_apply(n, b, f_rstd, f_tr, n - 1, f_xn)

            def ffn_xt(n, b):
                need(dve, f_tr, n + 1)
                need(dve, f_u, (n - 1) * 2)
                dve.tensor_copy(xT[:, b, :, :].rearrange("p c t -> p (c t)"), PM[:, :]).then_inc(f_xt, 1)

            def ffn_out(n, b):
                need(dve, f_d, n + 1)
                need(dve, f_y, n - 1)
                for c in range(CH):
                    bias = WX[b][:, CH * FF + FT * E + FT + c:CH * FF + FT * E + FT + c + 1]
                    dve.tensor_scalar(rT[b][:, c * S:(c + 1) * S], PO[:, c * S:(c + 1) * S], bias, None,
                                      ALU.add).then_inc(f_r, 1)

            def ffn_fin(n, b, m):
                need(dve, f_base, (n + 1) * TT)
                need(dve, f_out[b], m * 16)
                for tt in range(TT):
                    tt_(fin[b][:, tt * E:(tt + 1) * E], h_row(n, tt), bo3, ALU.add)
                dve.drain()
                need(dve, f_y, n + 1)
                for tt in range(TT):
                    f = fin[b][:, tt * E:(tt + 1) * E]
                    dve.scalar_tensor_tensor(out=f, in0=y_ps(b)[:, tt * E:(tt + 1) * E], scalar=0.3, in1=f,
                                             op0=ALU.mult, op1=ALU.add).then_inc(f_fin, 1)

            def ffn(n, b, m):
                ffn_in(n + 1, 1 - b)
                ffn_xt(n + 1, 1 - b)
                ffn_out(n, b)
                ffn_fin(n, b, m)

            ffn_in(0, 0)
            ffn_xt(0, 0)
            images(dve, ffn, B - 1)
            ffn_out(B - 1, 1)
            ffn_fin(B - 1, 1, B // 2 - 1)

        @block.tensor
        def _(pe):
            mm = pe.matmul

            pe.wait_ge(s_cst, 18)
            with pe.Fori(0, TILES) as t:
                pe.wait_ge(s_part, t + 1)
                mm(PM[:, 0:10], blkones[:, :], part, start=True, stop=True).then_inc(s_zps, 1)

            def scores_max(v, kv, lap, g):
                r = kv % RING
                if g == 0:
                    need(pe, s_qp[r], (lap + kv // RING + 1) * 96)
                need(pe, s_mx, v * 4 + 2 * g)
                for hh in range(0, GH, 2):
                    dst = S1[:, hh * S:(hh + 2) * S].rearrange("p (h q) -> p h q", h=2)[:, :, P:S]
                    mm(dst, identb[:, :], maskb[:, :].rearrange("p (o k) -> p o k", o=1).to_broadcast([P, 2, P]),
                       start=True, stop=False, skip_group_check=True)
                mm(S1[:, 1024:1536].rearrange("p (h q) -> p h q", h=GH), identb[:, :],
                   maskb[:, :].rearrange("p (o k) -> p o k", o=1).to_broadcast([P, GH, P]),
                   start=True, stop=False, skip_group_check=True)
                for j in range(GH):
                    h = GH * g + j
                    mm(S1[:, j * S:(j + 1) * S], QP[0:KQ, r, h, P:S], KP[0:KQ, r, h, :],
                       start=False, stop=True, skip_group_check=True)
                for j in range(GH):
                    h = GH * g + j
                    ins = mm(S1[:, 1024 + j * P:1024 + (j + 1) * P], QP[0:KQ, r, h, 0:P], KP[0:KQ, r, h, 0:P],
                             start=False, stop=True, skip_group_check=True)
                ins.then_inc(s_p1, 1)

            def scores_exp(u, k, g):
                if g == 0:
                    need(pe, s_mrow, (u + 1) * 48)
                need(pe, s_exp, u * 2 + g)
                for j in range(GH):
                    h = GH * g + j
                    mm(S2[:, j * S:(j + 1) * S], KP[0:KM, k % RING, h, 0:P], QP[0:KM, k % RING, h, :],
                       start=True, stop=True)
                for j in range(GH):
                    h = GH * g + j
                    ins = mm(S2[:, 1024 + j * P:1024 + (j + 1) * P], KP[0:KM, k % RING, h, P:S],
                             QP[0:KM, k % RING, h, P:S], start=True, stop=True)
                ins.then_inc(s_p2, 1)

            def weighted(u, n, k, g):
                if g == 0:
                    need(pe, s_os, u)
                    need(pe, s_va, n + 1)
                need(pe, s_sel, u * 4 + 2 * (g + 1))
                vb = Va[:, (k // 2) % 2, :, :, :, :]
                for kt in range(TT):
                    for j in range(GH):
                        h = (k % 2) * HU + GH * g + j
                        if kt == 0:
                            dst, pr = PO[32 * j:32 * j + 32, g * S:(g + 1) * S], PT[:, g, j * S:(j + 1) * S]
                        else:
                            dst = PO[32 * j:32 * j + 32, g * S + P:(g + 1) * S]
                            pr = PT[:, g, 1024 + j * P:1024 + (j + 1) * P]
                        ins = mm(dst, vb[:, kt, h, :, :].rearrange("p d c -> p (d c)"), pr,
                                 start=(kt == 0), stop=(kt == 1), skip_group_check=True)
                ins.then_inc(s_pv, 1)

            def slot(u, n, k, lap):
                v, w, odd = u + 1, u + 3, k % 2
                if unit_ok(v):
                    scores_max(v, k + 1, lap, 0)
                if unit_ok(w):
                    b = (k + 3) % 2
                    xb = ((k + 3) // 2) % 2
                    if odd:
                        need(pe, s_xt, n + 3)
                    else:
                        if unit_ok(u):
                            need(pe, s_mf, u + 1)
                        else:
                            need(pe, s_qa, u + 3)
                        need(pe, s_xt, n + 2)
                    for o in range(2):
                        for c in range(CH):
                            ins = mm(PM[:, o * S:(o + 1) * S], w1_sb[:, c, o, b * P:(b + 1) * P], xT[:, xb, c, :],
                                     start=(c == 0), stop=(c == CH - 1))
                    ins.then_inc(s_d, 1)
                if unit_ok(v):
                    scores_max(v, k + 1, lap, 1)
                if unit_ok(u):
                    scores_exp(u, k, 0)
                if not odd and image_ok(n + 1):
                    need(pe, s_qa, u + 4)
                    need(pe, s_xt, n + 2)
                    for tt in range(TT):
                        for c in range(CH):
                            ins = mm(PM[:, tt * E:(tt + 1) * E], xT[:, (k // 2 + 1) % 2, c, tt * P:(tt + 1) * P],
                                     w1_sb[:, c, 2, :], start=(c == 0), stop=(c == CH - 1))
                    ins.then_inc(s_v, 1)
                if odd and image_ok(n - 1):
                    if unit_ok(w):
                        need(pe, s_qa, u + 4)
                    else:
                        need(pe, s_mf, min(u + 1, UNITS))
                        need(pe, s_h2, n - 1)
                    need(pe, s_ac, n * 2)
                    for tt in range(TT):
                        for c in range(UPI):
                            ins = mm(PM[:, tt * E:(tt + 1) * E],
                                     AC[:, ((k // 2 - 1) * 2 + c) % RING, tt * P:(tt + 1) * P],
                                     wp_sb[:, c, :], start=(c == 0), stop=(c == UPI - 1))
                    ins.then_inc(s_wp, 1)
                if unit_ok(v):
                    need(pe, s_mx, v * 4 + 4)
                    if odd:
                        if image_ok(n - 1):
                            need(pe, s_h2, n)
                        else:
                            need(pe, s_qa, u + 4)
                    else:
                        if image_ok(n + 1):
                            need(pe, s_va, n + 2)
                        elif unit_ok(w):
                            need(pe, s_qa, u + 4)
                        else:
                            need(pe, s_mf, u + 1)
                    pe.transpose(PM[0:TT * HU, 0:P], mx[:, (k + 1) % 2, :], ident[:, :]).then_inc(s_mt, 1)
                if unit_ok(u):
                    scores_exp(u, k, 1)
                    weighted(u, n, k, 0)
                if not odd and image_ok(n + 2):
                    if unit_ok(v):
                        need(pe, s_mf, u + 2)
                    elif image_ok(n + 1):
                        need(pe, s_va, n + 2)
                    elif unit_ok(w):
                        need(pe, s_qa, u + 4)
                    need(pe, s_xn, n + 3)
                    for c in range(CH):
                        for tt in range(TT):
                            ins = pe.transpose(PM[:, c * S + tt * P:c * S + (tt + 1) * P],
                                               xn[:, (k // 2) % 2, tt, c * P:(c + 1) * P], ident[:, :])
                    ins.then_inc(s_tr, 1)
                if unit_ok(u):
                    weighted(u, n, k, 1)

            pe.wait_ge(s_wts, 16 * 5)
            slots(pe, slot)

            pe.wait_ge(f_ln, 1)
            pe.wait_ge(s_h2, B)
            for c in range(CH):
                ins = pe.transpose(PM[:, c * B:(c + 1) * B], lastr[0:B, c * P:(c + 1) * P], ident[0:B, 0:B])
            ins.then_inc(f_lt, 1)
            pe.wait_ge(f_lte, 1)
            pe.wait_ge(f_w, 16 * 6)
            for c in range(CH):
                ins = mm(PM[:, 0:B], wp1_sb[:, c * NAV:(c + 1) * NAV], lastT[:, c * B:(c + 1) * B],
                         start=(c == 0), stop=(c == CH - 1))
            ins.then_inc(f_ga, 1)
            pe.wait_ge(f_gae, 1)
            mm(PM[0:B, 0:NX], gact, wp2_sb, start=True, stop=True).then_inc(f_lg, 1)
            pe.wait_ge(f_idx, 1)

            def ffn_tr(n, b):
                need(pe, f_xn, n + 1)
                need(pe, f_xt, n)
                for c in range(CH):
                    for tt in range(TT):
                        ins = pe.transpose(PM[:, c * S + tt * P:c * S + (tt + 1) * P], xn[:, b, tt, c * P:(c + 1) * P],
                                           ident[:, :])
                ins.then_inc(f_tr, 1)

            def ffn_up(n, b, m):
                need(pe, f_xt, n + 1)
                pe.wait_ge(f_wx[b], (m + 1) * 16)
                need(pe, f_g, (n - 1) * FT)
                for f in range(FT):
                    for c in range(CH):
                        ins = mm((S1 if b == 0 else S2)[:, f * S:(f + 1) * S],
                                 WX[b][:, c * FF + f * P:c * FF + (f + 1) * P], xT[:, b, c, :],
                                 start=(c == 0), stop=(c == CH - 1))
                    if f % 2:
                        ins.then_inc(f_u, 1)

            def ffn_down(n, b):
                need(pe, f_g, (n + 1) * FT)
                need(pe, f_r, n * CH)
                for c in range(CH):
                    for f in range(FT):
                        w0 = CH * FF + f * E + c * P
                        ins = mm(PO[:, c * S:(c + 1) * S], WX[b][:, w0:w0 + P], gT[b][:, f * S:(f + 1) * S],
                                 start=(f == 0), stop=(f == FT - 1))
                ins.then_inc(f_d, 1)

            def ffn_y(n, b):
                need(pe, f_r, (n + 1) * CH)
                need(pe, f_fin, (n - 1) * TT)
                for tt in range(TT):
                    for c in range(CH):
                        ins = mm(y_ps(b)[:, tt * E:(tt + 1) * E], rT[b][:, c * S + tt * P:c * S + (tt + 1) * P],
                                 wo_sb[:, c * E:(c + 1) * E], start=(c == 0), stop=(c == CH - 1))
                ins.then_inc(f_y, 1)

            def ffn(n, b, m):
                ffn_tr(n + 1, 1 - b)
                ffn_down(n, b)
                ffn_up(n + 1, 1 - b, m + b)
                ffn_y(n, b)

            ffn_tr(0, 0)
            ffn_up(0, 0, 0)
            images(pe, ffn, B - 1)
            ffn_down(B - 1, 1)
            ffn_y(B - 1, 1)


def layouts(a):
    c = np.ascontiguousarray
    img = a["x"].reshape(TILES, P, 8 * E)
    fine = []
    for name, (r, w) in zip(("L0_tok_Wd3", "L0_tok_Wd2", "L0_tok_Wd1"), LVL):
        fine.append(a[name].reshape(3, BLK, r, w, 3).transpose(1, 4, 0, 2, 3).reshape(BLK, -1))
    wd = np.concatenate(fine + [a["L0_tok_Wa"].reshape(BLK, -1)], axis=1)
    bd = np.concatenate([a["L0_tok_bd3"], a["L0_tok_bd2"], a["L0_tok_bd1"], a["L0_tok_ba"]]).reshape(1, 10)
    w1 = a["L0_attn_W1"].reshape(CH, P, H, 3, D)
    qk = w1[:, :, :, 0:2].reshape(CH, P, UPI, HU, 2, D).transpose(1, 0, 4, 2, 5, 3).reshape(P, CH, 2, E)
    v = w1[:, :, :, 2].transpose(1, 0, 2, 3).reshape(P, CH, 1, E)
    b1 = a["L0_attn_b1"].reshape(H, 3, D)
    bqk = b1[:, 0:2].reshape(UPI, HU, 2, D).transpose(3, 1, 0, 2).reshape(P, UPI, 2)
    wp = a["L0_attn_Wp"].reshape(UPI, 2, GH, D, E).transpose(2, 3, 1, 0, 4).reshape(P, UPI, E)
    wx = np.concatenate([
        a["L0_ffn_W1"].reshape(NX, CH, P, FF).transpose(0, 2, 1, 3).reshape(NX, P, -1),
        a["L0_ffn_W2"].reshape(NX, FT, P, E).transpose(0, 2, 1, 3).reshape(NX, P, -1),
        a["L0_ffn_b1"].reshape(NX, FT, P).transpose(0, 2, 1),
        a["L0_ffn_b2"].reshape(NX, CH, P).transpose(0, 2, 1)], axis=2)
    rows = lambda m: m.reshape(-1, P, m.shape[1]).transpose(1, 0, 2).reshape(P, -1)
    return {
        "x": c(img), "wd": c(wd), "bd": c(bd), "w1": c(np.concatenate([qk, v], axis=2)), "bqk": c(bqk),
        "bv": c(b1[:, 2].reshape(1, E)), "wp": c(wp), "bp": c(a["L0_attn_bp"].reshape(1, E)),
        "wp1": c(rows(a["L0_ffn_Wp1"])), "bp1": c(a["L0_ffn_bp1"].reshape(P, 1)), "wp2": c(a["L0_ffn_Wp2"]),
        "bp2": c(a["L0_ffn_bp2"].reshape(1, NX)), "wx": c(wx), "wo": c(rows(a["L0_ffn_Wo"])),
        "bo": c(a["L0_ffn_bo"].reshape(1, E)),
    }


def kernel(**inputs):
    import concourse.bacc as bacc
    from concourse.bass_utils import run_bass_kernel_spmd

    nc = bacc.Bacc("TRN2", target_bir_lowering=False, num_devices=1)
    arrays = layouts({k: np.asarray(v) for k, v in inputs.items()})
    args = {k: nc.dram_tensor(f"in_{k}", v.shape, mybir.dt.from_np(v.dtype), kind="ExternalInput").ap()
            for k, v in arrays.items()}
    args["out"] = nc.dram_tensor("out_h", (B, S, E), F32, kind="ExternalOutput").ap()
    tower(nc, **args)
    r = run_bass_kernel_spmd(nc, [{f"in_{k}": v for k, v in arrays.items()}], core_ids=[0])
    return r.results[0]["out_h"]
```

```python
from contextlib import ExitStack

import numpy as np

import concourse.bass as bass
from concourse import mybir

F32 = mybir.dt.float32
BF16 = mybir.dt.bfloat16
U32 = mybir.dt.uint32
ALU = mybir.AluOpType
ACT = mybir.ActivationFunctionType
AX = mybir.AxisListType.X

P = 128
B, S, E = 16, 256, 256
H, D = 16, 16
NX, FF, NAV = 8, 512, 128
TT, CH, FT = S // P, E // P, FF // P
EPS = 1e-5
BLK = S // 8
IPT = P // BLK
TILES = B // IPT
UPI = 2
HU = H // UPI
UNITS = B * UPI
GH = 4
SLOTS = 6
KQ = SLOTS * D
KM = KQ + 2
RING = 4
BIG = -1.0e6
LVL = ((4, 128), (2, 64), (1, 32))
LW = [3 * r * c for r, c in LVL]
WD_OFF = [0, 3 * LW[0], 3 * (LW[0] + LW[1]), 3 * sum(LW)]
WD_W = 3 * sum(LW) + LVL[2][0] * LVL[2][1]
WX_W = CH * FF + FT * E + FT + CH


def tower(nc, x, wd, bd, w1, bqk, bv, wp, bp, wp1, bp1, wp2, bp2, wx, wo, bo, out):
    bounce = nc.dram_tensor("bounce", [RING, 2, 3, P, S], BF16).ap()
    with ExitStack() as ctx:
        def sb(name, shape, dt=F32):
            return ctx.enter_context(nc.sbuf_tensor(name, shape, dt))

        def sem(name):
            return ctx.enter_context(nc.semaphore(name))

        S1 = ctx.enter_context(nc.psum_tensor("S1", [P, 1536], F32))
        S2 = ctx.enter_context(nc.psum_tensor("S2", [P, 1536], F32))
        PO = ctx.enter_context(nc.psum_tensor("PO", [P, 512], F32))
        PM = ctx.enter_context(nc.psum_tensor("PM", [P, 512], F32))

        hN = sb("hN", [P, B * TT, E])
        ident = sb("ident", [P, P])
        identb = sb("identb", [P, P], BF16)
        maskb = sb("maskb", [P, P], BF16)
        blkones = sb("blkones", [P, P])
        half = sb("half", [P, 2])
        stat = sb("stat", [P, 2, TT, 6])
        mv = sb("mv", [P, 2, TT, 2])
        ve = sb("ve", [P, 2, TT])
        rstd = sb("rstd", [P, 2, TT])
        xn = sb("xn", [P, 2, TT, E])
        xT = sb("xT", [P, 2, CH, S])
        arena = sb("arena", [P, 15700])
        cur = [0]

        def carve(n):
            a = arena[:, cur[0]:cur[0] + n]
            cur[0] += n
            return a

        X = carve(8 * E)
        LO = [carve(2 * r * c) for r, c in LVL]
        HI = [carve(2 * r * c) for r, c in LVL]
        DT = [carve(n) for n in LW]
        AA = [carve(r * c) for r, c in LVL]
        REC = [X, AA[0], AA[1]]
        RX = carve(8 * E)
        WD = carve(WD_W)
        part = carve(10)
        z = carve(10)
        ez = carve(10)
        es = carve(10)
        zmax = carve(3)
        zsum = carve(4)
        zrec = carve(4)
        wg = carve(10)
        bdt = carve(10)
        wscale = carve(10)
        assert cur[0] <= 15700
        cur[0] = 0
        WX = [carve(WX_W) for _ in range(2)]
        gT = [carve(FT * S) for _ in range(2)]
        rT = [carve(CH * S) for _ in range(2)]
        fin = [carve(TT * E) for _ in range(2)]
        wo_sb = carve(CH * E)
        bo3 = carve(E)
        wp1_sb = carve(CH * NAV)
        wp2_sb = carve(NX)
        bp1_sb = carve(1)
        bp2_sb = carve(NX)
        lastr = carve(E)
        lstat = carve(6)
        lmv = carve(2)
        lve = carve(1)
        lrstd = carve(1)
        lastT = carve(CH * B)
        gact = carve(B)
        logit = carve(NX)
        top8 = carve(NX)
        assert cur[0] <= 15700
        idx8 = sb("idx8", [B, 8], U32)
        idxr = sb("idxr", [1, B], U32)

        w1_sb = sb("w1_sb", [P, CH, 3, E])
        wp_sb = sb("wp_sb", [P, UPI, E])
        bqk_sb = sb("bqk_sb", [P, UPI, 2])
        bv_sb = sb("bv_sb", [P, E])
        bp_sb = sb("bp_sb", [P, E])
        QF = sb("QF", [P, 2, 2, S])
        QR = sb("QR", [P, 2, 2, S])
        QB = sb("QB", [P, 2, 2, 3, S], BF16)
        QP = sb("QP", [P, RING, HU, S], BF16)
        KP = sb("KP", [P, RING, HU, S], BF16)
        Va = sb("Va", [P, 2, TT, H, D, 2])
        PT = sb("PT", [P, 2, 1536])
        OS = sb("OS", [P, 2, 2, S])
        AU = sb("AU", [P, 2, S])
        SC = sb("SC", [P, 2, S])
        AC = sb("AC", [P, RING, S])
        mx = sb("mx", [P, 2, TT * HU])
        mB = sb("mB", [TT * HU, 2, 2, P], BF16)

        s_cst = sem("s_cst")
        s_x = sem("s_x")
        s_wd = sem("s_wd")
        s_wts = sem("s_wts")
        s_xfree = sem("s_xfree")
        s_part = sem("s_part")
        s_zps = sem("s_zps")
        s_z = sem("s_z")
        s_ez = sem("s_ez")
        s_wg = sem("s_wg")
        s_gate = sem("s_gate")
        s_rec = sem("s_rec")
        s_h0 = sem("s_h0")
        s_stat = sem("s_stat")
        s_rstd = sem("s_rstd")
        s_xn = sem("s_xn")
        s_bp = sem("s_bp")
        s_tr = sem("s_tr")
        s_xt = sem("s_xt")
        s_d = sem("s_d")
        s_qa = sem("s_qa")
        s_hi = sem("s_hi")
        s_r1 = sem("s_r1")
        s_mid = sem("s_mid")
        s_lo = sem("s_lo")
        s_scr = sem("s_scr")
        s_qp = [sem(f"s_qp{r}") for r in range(RING)]
        s_p1 = sem("s_p1")
        s_mx = sem("s_mx")
        s_mt = sem("s_mt")
        s_ms = sem("s_ms")
        s_mrow = sem("s_mrow")
        s_p2 = sem("s_p2")
        s_exp = sem("s_exp")
        s_sel = sem("s_sel")
        s_pv = sem("s_pv")
        s_os = sem("s_os")
        s_oc = [sem(f"s_oc{b}") for b in range(2)]
        s_ac = sem("s_ac")
        s_v = sem("s_v")
        s_va = sem("s_va")
        s_wp = sem("s_wp")
        s_h2 = sem("s_h2")
        s_turn = sem("s_turn")
        sp_turn = sem("sp_turn")
        f_w = sem("f_w")
        f_last = sem("f_last")
        f_lst = sem("f_lst")
        f_lrs = sem("f_lrs")
        f_ln = sem("f_ln")
        f_lt = sem("f_lt")
        f_lte = sem("f_lte")
        f_ga = sem("f_ga")
        f_gae = sem("f_gae")
        f_lg = sem("f_lg")
        f_idx = sem("f_idx")
        f_idr = sem("f_idr")
        f_wx = [sem(f"f_wx{b}") for b in range(2)]
        f_stat = sem("f_stat")
        f_rstd = sem("f_rstd")
        f_xn = sem("f_xn")
        f_base = sem("f_base")
        f_tr = sem("f_tr")
        f_xt = sem("f_xt")
        f_u = sem("f_u")
        f_g = sem("f_g")
        f_d = sem("f_d")
        f_r = sem("f_r")
        f_y = sem("f_y")
        f_fin = sem("f_fin")
        f_out = [sem(f"f_out{b}") for b in range(2)]

        def need(eng, s, v):
            if not isinstance(v, int) or v > 0:
                eng.wait_ge(s, v)

        def h_row(n, tt):
            return hN[:, bass.ds(n * TT + tt, 1), :].rearrange("p o e -> p (o e)")

        def bcast(ap, shape):
            return ap.to_broadcast(shape)

        FIRST, LAST = -3 * UPI, UNITS + 1
        LOOP0, LOOPS = 4, 5

        def slots(eng, body):
            for u in range(FIRST, LOOP0):
                body(u, u // 2, u, 0)
            with eng.Fori(0, LOOPS) as it:
                for k in range(4):
                    body(it * 4 + (LOOP0 + k), it * 2 + (LOOP0 + k) // 2, k, it + LOOP0 // RING)
            for u in range(LOOP0 + 4 * LOOPS, LAST + 1):
                body(u, u // 2, u, 0)

        def images(eng, body, count):
            turns = (B - 2) // 2
            for n in range(2):
                body(n, n, 0)
            with eng.Fori(1, turns) as it:
                for b in range(2):
                    body(it * 2 + b, b, it)
            for n in range(turns * 2, count):
                body(n, n % 2, n // 2)

        def unit_ok(u):
            return not isinstance(u, int) or 0 <= u < UNITS

        def image_ok(n):
            return not isinstance(n, int) or 0 <= n < B

        def y_ps(b):
            return (S1 if b == 0 else S2)[:, 1024:1536]

        block = ctx.enter_context(nc.Block())

        @block.gpsimd
        def _(pool):
            pool.memset(ident[:, :], 0.0).then_inc(s_cst, 1)
            pool.memset(identb[:, :], 0.0).then_inc(s_cst, 1)
            pool.memset(maskb[:, :], 0.0).then_inc(s_cst, 1)
            pool.memset(blkones[:, :], 0.0).then_inc(s_cst, 1)
            pool.memset(half[:, :], -0.5).then_inc(s_cst, 1)
            pool.wait_ge(s_cst, 5)
            pool.memset(KP[96:P, :, :, :], 1.0).then_inc(s_cst, 1)
            pool.wait_ge(s_cst, 6)
            pool.memset(Va[:, :, :, :, :, 1], 1.0).then_inc(s_cst, 1)
            for l in range(3):
                pool.memset(wscale[:, 3 * l:3 * l + 3], 0.25 ** (l + 1)).then_inc(s_cst, 1)
            pool.memset(wscale[:, 9:10], 0.25 ** 3).then_inc(s_cst, 1)
            pool.wait_ge(s_cst, 11)
            for m in (ident, identb):
                pool.affine_select(out=m[:, :], in_=m[:, :], compare_op=ALU.not_equal, fill=1.0, base=0,
                                   pattern=[[-1, P]], channel_multiplier=1).then_inc(s_cst, 1)
            pool.affine_select(out=maskb[:, :], in_=maskb[:, :], compare_op=ALU.is_ge, fill=BIG, base=0,
                               pattern=[[-1, P]], channel_multiplier=1).then_inc(s_cst, 1)
            for i in range(IPT):
                pool.wait_ge(s_cst, 14 + i)
                pool.memset(blkones[BLK * i:BLK * i + BLK, BLK * i:BLK * i + BLK], 1.0).then_inc(s_cst, 1)

            def slot(u, n, k, lap):
                w, odd = u + 4, k % 2
                if unit_ok(u):
                    select(u, 0)
                if unit_ok(w):
                    need(pool, s_hi, w + 1)
                    need(pool, s_lo, w - 1)
                    pool.tensor_tensor(QR[:, odd, :, :], QF[:, odd, :, :], QB[:, odd, :, 0, :],
                                       ALU.subtract).then_inc(s_r1, 1)
                if unit_ok(u):
                    select(u, 1)
                if unit_ok(w):
                    need(pool, s_mid, w + 1)
                    pool.tensor_tensor(QB[:, odd, :, 2, :], QR[:, odd, :, :], QB[:, odd, :, 1, :],
                                       ALU.subtract).then_inc(s_lo, 1)
                if not odd and image_ok(n + 3):
                    b = (k // 2 + 3) % 2
                    need(pool, s_stat, n + 4)
                    pool.tensor_tensor(rstd[:, b, :], ve[:, b, :], half[:, :], ALU.pow).then_inc(s_rstd, 1)
                if odd and image_ok(n + 3):
                    need(pool, s_xn, (n + 4) * TT)
                    for tt in range(TT):
                        a = h_row(n + 3, tt)
                        pool.tensor_tensor(a, a, bp_sb[:, :], ALU.add).then_inc(s_bp, 1)

            def select(u, g):
                need(pool, s_exp, u * 2 + (g + 1))
                pool.sem_inc(s_turn, 1)
                pt = PT[:, g, :]
                for v in (pt[:, 0:1024].rearrange("p (h q) -> p h q", h=GH)[:, :, 0:P],
                          pt[:, 1024:1536].rearrange("p (h q) -> p h q", h=GH)):
                    pool.affine_select(out=v, in_=v, compare_op=ALU.is_ge, fill=0.0, base=0,
                                       pattern=[[0, GH], [1, P]], channel_multiplier=-1).then_inc(s_sel, 1)

            pool.wait_ge(s_cst, 18)
            pool.wait_ge(s_wts, 16 * 5)
            slots(pool, slot)

            pool.wait_ge(f_lst, 1)
            pool.tensor_tensor(lrstd[0:B, :], lve[0:B, :], half[0:B, 0:1], ALU.pow).then_inc(f_lrs, 1)

            def ffn(n, b, m):
                need(pool, f_stat, n + 1)
                pool.tensor_tensor(rstd[:, b, :], ve[:, b, :], half[:, :], ALU.pow).then_inc(f_rstd, 1)
                need(pool, f_xn, (n + 1) * TT)
                for tt in range(TT):
                    a = h_row(n, tt)
                    pool.tensor_tensor(a, a, xn[:, b, tt, :], ALU.add).then_inc(f_base, 1)

            images(pool, ffn, B)

        @block.sync
        def _(sp):
            def need_sp(s, v):
                need(sp, s, v)
                if not isinstance(v, int):
                    sp.sem_inc(sp_turn, 1)

            sp.dma_start(X, x[0]).then_inc(s_x, 16)
            for i in range(IPT):
                sp.dma_start(WD[BLK * i:BLK * i + BLK, :], wd).then_inc(s_wd, 16)
            sp.dma_start(bdt, bcast(bd, [P, 10])).then_inc(s_wd, 16)
            sp.dma_start(w1_sb[:, :, :, :], w1).then_inc(s_wts, 16)
            sp.dma_start(wp_sb[:, :, :], wp).then_inc(s_wts, 16)
            sp.dma_start(bqk_sb[:, :, :], bqk).then_inc(s_wts, 16)
            sp.dma_start(bv_sb[:, :], bcast(bv, [P, E])).then_inc(s_wts, 16)
            sp.dma_start(bp_sb[:, :], bcast(bp, [P, E])).then_inc(s_wts, 16)

            def rows_out(t):
                need_sp(s_rec, t + 1)
                for i in range(IPT):
                    for tt in range(TT):
                        p0 = BLK * i + BLK // TT * tt
                        sp.dma_start(h_row(t * IPT + i, tt),
                                     RX[p0:p0 + BLK // TT, :].rearrange("p (r e) -> p r e", r=8)).then_inc(s_h0, 16)

            with sp.Fori(0, TILES - 1) as t:
                need_sp(s_xfree, t + 1)
                sp.dma_start(X, x[bass.ds(t + 1, 1)].rearrange("o p c -> (o p) c")).then_inc(s_x, 16)
                rows_out(t)
            rows_out(TILES - 1)

            def slot(u, n, k, lap):
                v, w = u + 1, u + 3
                if unit_ok(u - 1):
                    b = (k - 1) % 2
                    need_sp(s_os, u)
                    need_sp(s_ac, u - 2)
                    for c, dst in ((0, AU), (1, SC)):
                        sp.dma_start(dst[:, b, :], OS[c:P:2, b, :, :]).then_inc(s_oc[b], 16)
                if unit_ok(w):
                    r = (k + 3) % RING
                    need_sp(s_scr, (w + 1) * 16)
                    need_sp(s_p2, (w - 3) * 2)
                    for o, dst, plan in ((0, QP, ((0, 0, 3, 3), (3, 0, 2, 2), (5, 0, 1, 1))),
                                         (1, KP, ((0, 0, 1, 3), (3, 1, 1, 2), (5, 2, 1, 1)))):
                        for at, part0, parts, count in plan:
                            src = bounce[r, o, part0:part0 + parts].rearrange("s (d h) t -> (s d) (h t)", h=HU)
                            if parts < count:
                                src = bounce[r, o, part0:part0 + 1].rearrange(
                                    "s (d h) t -> s d (h t)", h=HU).to_broadcast([count, D, HU * S])
                            sp.dma_start(dst[at * D:(at + count) * D, r, :, :], src).then_inc(s_qp[r], 16)
                if unit_ok(v):
                    need_sp(s_ms, v + 1)
                    for s in range(2):
                        sp.dma_start(QP[KQ + s:KQ + s + 1, (k + 1) % RING, :, :].rearrange(
                            "p h (t q) -> p (h t) q", t=TT), mB[:, (k + 1) % 2, s, :]).then_inc(s_mrow, 16)
                w = u + 4
                if unit_ok(w):
                    need_sp(s_lo, w + 1)
                    need_sp(s_qp[k % RING], (lap + (k + 4) // RING) * 96)
                    sp.dma_start(bounce[k % RING].rearrange("o s p t -> p (o s) t"),
                                 QB[:, k % 2, :, :, :].rearrange("p o s t -> p (o s) t")).then_inc(s_scr, 16)

            slots(sp, slot)

            sp.wait_ge(s_h0, 16 * B * TT)
            sp.dma_start(wo_sb, wo).then_inc(f_w, 16)
            sp.dma_start(bo3, bcast(bo, [P, E])).then_inc(f_w, 16)
            sp.dma_start(wp1_sb, wp1).then_inc(f_w, 16)
            sp.dma_start(wp2_sb, wp2).then_inc(f_w, 16)
            sp.dma_start(bp1_sb, bp1).then_inc(f_w, 16)
            sp.dma_start(bp2_sb[0:B, :], bcast(bp2, [B, NX])).then_inc(f_w, 16)
            sp.wait_ge(s_h2, B)
            sp.dma_start(lastr[0:B, :], hN[P - 1:P, 1:B * TT:TT, :]).then_inc(f_last, 16)
            sp.wait_ge(f_idx, 1)
            sp.dma_start(idxr[:, :], idx8[:, 0:1]).then_inc(f_idr, 16)
            sp.wait_ge(f_idr, 16)

            def load_expert(n, b):
                need_sp(f_d, n - 1)
                need_sp(f_r, (n - 1) * CH)
                e = sp.value_load(idxr[0:1, bass.ds(n, 1)], min_val=0, max_val=NX - 1)
                sp.dma_start(WX[b], wx[bass.ds(e, 1)].rearrange("o p c -> (o p) c")).then_inc(f_wx[b], 16)

            def store(n, b):
                need_sp(f_fin, (n + 1) * TT)
                sp.dma_start(out[bass.ds(n, 1)].rearrange("o (t p) e -> p (o t) e", p=P),
                             fin[b].rearrange("p (t e) -> p t e", t=TT)).then_inc(f_out[b], 16)

            def ffn(n, b, m):
                load_expert(n + 1, 1 - b)
                if not isinstance(n, int) or n > 0:
                    store(n - 1, 1 - b)

            load_expert(0, 0)
            images(sp, ffn, B - 1)
            store(B - 2, 0)
            store(B - 1, 1)
            for b in range(2):
                sp.wait_ge(f_out[b], 16 * (B // 2))

        @block.scalar
        def _(act):
            dt3 = [DT[l].rearrange("p (k n) -> p k n", k=3) for l in range(3)]
            with act.Fori(0, TILES) as t:
                act.wait_ge(s_z, t + 1)
                nc.scalar.activation(ez, z, ACT.Exp).then_inc(s_ez, 1)
                act.wait_ge(s_wg, t + 1)
                nc.scalar.activation(AA[2], AA[2], ACT.Copy, scale=wg[:, 9:10]).then_inc(s_gate, 1)
                for l in (2, 1, 0):
                    for c in range(3):
                        nc.scalar.activation(dt3[l][:, c, :], dt3[l][:, c, :], ACT.Copy,
                                             scale=wg[:, 3 * l + c:3 * l + c + 1]).then_inc(s_gate, 1)

            def slot(u, n, k, lap):
                w, odd = u + 4, k % 2
                if unit_ok(u):
                    exponential(u, 0)
                if unit_ok(w):
                    need(act, s_d, w + 1)
                    need(act, s_lo, w - 1)
                    for o in range(2):
                        nc.scalar.activation(QF[:, odd, o, :], PM[:, o * S:(o + 1) * S], ACT.Identity,
                                             bias=bqk_sb[:, odd, o:o + 1]).then_inc(s_qa, 1)
                if unit_ok(u):
                    exponential(u, 1)
                if unit_ok(u):
                    need(act, s_pv, u * 2 + 2)
                    need(act, s_oc[k % 2], n * 32)
                    nc.scalar.copy(OS[:, k % 2, :, :].rearrange("p g t -> p (g t)"), PO[:, :]).then_inc(s_os, 1)
                if odd and image_ok(n + 3):
                    need(act, s_tr, n + 4)
                    need(act, s_v, n + 2)
                    need(act, s_d, u + 3)
                    nc.scalar.copy(xT[:, (k // 2 + 3) % 2, :, :].rearrange("p c t -> p (c t)"),
                                   PM[:, :]).then_inc(s_xt, 1)

            def exponential(u, g):
                need(act, s_p2, u * 2 + (g + 1))
                need(act, s_pv, u * 2 + (g - 1))
                nc.scalar.activation(PT[:, g, :], S2[:, :], ACT.Exp, scale=float(D) ** -0.5).then_inc(s_exp, 1)

            slots(act, slot)

            act.wait_ge(f_ga, 1)
            act.wait_ge(f_w, 16 * 6)
            nc.scalar.activation(gact, PM[:, 0:B], ACT.Gelu, bias=bp1_sb).then_inc(f_gae, 1)

            def ffn(n, b, m):
                for j in range(2):
                    need(act, f_u, n * 2 + (j + 1))
                    if j == 0:
                        need(act, f_d, n - 1)
                    act.wait_ge(f_wx[b], (m + 1) * 16)
                    for c in range(2):
                        f = 2 * j + c
                        src = (S1 if b == 0 else S2)[:, f * S:(f + 1) * S]
                        nc.scalar.activation(gT[b][:, f * S:(f + 1) * S], src, ACT.Gelu,
                                             bias=WX[b][:, CH * FF + FT * E + f:CH * FF + FT * E + f + 1]).then_inc(f_g, 1)

            images(act, ffn, B)

        @block.vector
        def _(dve):
            tt_ = dve.tensor_tensor

            def analysis(src, l):
                r, c = LVL[l]
                s = src.rearrange("p (r c) -> p r c", r=2 * r)
                lo = LO[l].rearrange("p (r c) -> p r c", r=2 * r)
                hi = HI[l].rearrange("p (r c) -> p r c", r=2 * r)
                d = DT[l].rearrange("p (k r c) -> p k r c", k=3, r=r)
                a = AA[l].rearrange("p (r c) -> p r c", r=r)
                tt_(lo, s[:, :, 0::2], s[:, :, 1::2], ALU.add)
                ins = tt_(hi, s[:, :, 0::2], s[:, :, 1::2], ALU.subtract)
                dve.drain()
                tt_(a, lo[:, 0::2, :], lo[:, 1::2, :], ALU.add)
                tt_(d[:, 0], lo[:, 0::2, :], lo[:, 1::2, :], ALU.subtract)
                tt_(d[:, 1], hi[:, 0::2, :], hi[:, 1::2, :], ALU.add)
                tt_(d[:, 2], hi[:, 0::2, :], hi[:, 1::2, :], ALU.subtract)
                dve.drain()
                return ins

            def synthesis(dst, l):
                r, c = LVL[l]
                s = dst.rearrange("p (r c) -> p r c", r=2 * r)
                lo = LO[l].rearrange("p (r c) -> p r c", r=2 * r)
                hi = HI[l].rearrange("p (r c) -> p r c", r=2 * r)
                d = DT[l].rearrange("p (k r c) -> p k r c", k=3, r=r)
                a = AA[l].rearrange("p (r c) -> p r c", r=r)
                tt_(lo[:, 0::2, :], a, d[:, 0], ALU.add)
                tt_(lo[:, 1::2, :], a, d[:, 0], ALU.subtract)
                tt_(hi[:, 0::2, :], d[:, 1], d[:, 2], ALU.add)
                tt_(hi[:, 1::2, :], d[:, 1], d[:, 2], ALU.subtract)
                dve.drain()
                tt_(s[:, :, 0::2], lo, hi, ALU.add)
                return tt_(s[:, :, 1::2], lo, hi, ALU.subtract)

            dve.wait_ge(s_cst, 18)
            dve.wait_ge(s_wd, 16 * (IPT + 1))
            with dve.Fori(0, TILES) as t:
                dve.wait_ge(s_x, (t + 1) * 16)
                analysis(X, 0)
                dve.sem_inc(s_xfree, 1)
                analysis(AA[0], 1)
                analysis(AA[1], 2)
                need(dve, s_h0, t * (16 * IPT * TT))
                for l in range(3):
                    for j in range(3):
                        w0 = WD_OFF[l] + j * LW[l]
                        dve.tensor_tensor_reduce(RX[:, 0:LW[l]], DT[l], WD[:, w0:w0 + LW[l]], 0.5 ** (l + 1), 0.0,
                                                 ALU.mult, ALU.add, part[:, 3 * l + j:3 * l + j + 1])
                        dve.drain()
                na = LVL[2][0] * LVL[2][1]
                dve.tensor_tensor_reduce(RX[:, 0:na], AA[2], WD[:, WD_OFF[3]:WD_OFF[3] + na], 0.125, 0.0,
                                         ALU.mult, ALU.add, part[:, 9:10]).then_inc(s_part, 1)
                dve.wait_ge(s_zps, t + 1)
                tt_(z, PM[:, 0:10], bdt, ALU.add)
                dve.drain()
                z3 = z[:, 0:9].rearrange("p (l c) -> p l c", l=3)
                dve.tensor_reduce(zmax, z3, AX, ALU.max)
                dve.tensor_scalar(z[:, 9:10], z[:, 9:10], -1.0, None, ALU.mult)
                dve.drain()
                tt_(z3, z3, zmax.rearrange("p (l o) -> p l o", o=1).to_broadcast([P, 3, 3]),
                    ALU.subtract).then_inc(s_z, 1)
                dve.wait_ge(s_ez, t + 1)
                dve.tensor_reduce(zsum[:, 0:3], ez[:, 0:9].rearrange("p (l c) -> p l c", l=3), AX, ALU.add)
                dve.tensor_scalar(zsum[:, 3:4], ez[:, 9:10], 1.0, None, ALU.add)
                tt_(es[:, 0:9], ez[:, 0:9], wscale[:, 0:9], ALU.mult)
                dve.drain()
                dve.reciprocal(zrec, zsum)
                dve.drain()
                tt_(wg[:, 0:9].rearrange("p (l c) -> p l c", l=3), es[:, 0:9].rearrange("p (l c) -> p l c", l=3),
                    zrec[:, 0:3].rearrange("p (l o) -> p l o", o=1).to_broadcast([P, 3, 3]), ALU.mult)
                tt_(wg[:, 9:10], zrec[:, 3:4], wscale[:, 9:10], ALU.mult)
                dve.drain()
                dve.sem_inc(s_wg, 1)
                for l, gated in ((2, 4), (1, 7), (0, 10)):
                    dve.wait_ge(s_gate, t * 10 + gated)
                    ins = synthesis(RX if l == 0 else AA[l - 1], l)
                    if l:
                        dve.drain()
                ins.then_inc(s_rec, 1)
                dve.drain()

            def ln_stat(n, b, done):
                for tt in range(TT):
                    dve.bn_stats(stat[:, b, tt, :], h_row(n, tt))
                dve.drain()
                for tt in range(TT):
                    dve.bn_aggr(mv[:, b, tt, :], stat[:, b, tt, :])
                dve.drain()
                dve.tensor_scalar(ve[:, b, :], mv[:, b, :, 1], EPS, None, ALU.add).then_inc(done, 1)

            def ln_apply(n, b, rs, free, freed, done):
                need(dve, rs, n + 1)
                need(dve, free, freed)
                for tt in range(TT):
                    dve.tensor_scalar(xn[:, b, tt, :], h_row(n, tt), mv[:, b, tt, 0:1], rstd[:, b, tt:tt + 1],
                                      ALU.subtract, ALU.mult).then_inc(done, 1)

            def slot(u, n, k, lap):
                v, w, odd = u + 2, u + 4, k % 2
                b3 = (k // 2 + 3) % 2
                if unit_ok(u - 2):
                    need(dve, s_oc[odd], n * 32)
                    dve.reciprocal(SC[:, odd, :], SC[:, odd, :])
                    dve.drain()
                    need(dve, s_wp, n - 1)
                    tt_(AC[:, (k - 2) % RING, :], AU[:, odd, :], SC[:, odd, :], ALU.mult).then_inc(s_ac, 1)
                if not odd and image_ok(n + 3):
                    ln_stat(n + 3, b3, s_stat)
                if odd and image_ok(n + 3):
                    ln_apply(n + 3, b3, s_rstd, s_tr, n + 2, s_xn)
                if unit_ok(w):
                    need(dve, s_qa, (w + 1) * 2)
                    need(dve, s_scr, (w - 1) * 16)
                    dve.tensor_copy(QB[:, odd, :, 0, :], QF[:, odd, :, :]).then_inc(s_hi, 1)
                if unit_ok(v):
                    row_max(v, k + 2, 0)
                if unit_ok(u + 1):
                    b = (k + 1) % 2
                    need(dve, s_mt, u + 2)
                    need(dve, s_mrow, u * 32)
                    dve.tensor_scalar(mB[:, b, 0, :], PM[0:TT * HU, 0:P], -1.0, None, ALU.mult)
                    dve.drain()
                    dve.scalar_tensor_tensor(out=mB[:, b, 1, :], in0=PM[0:TT * HU, 0:P], scalar=-1.0,
                                             in1=mB[:, b, 0, :], op0=ALU.mult, op1=ALU.subtract).then_inc(s_ms, 1)
                if unit_ok(w):
                    need(dve, s_r1, w + 1)
                    dve.tensor_copy(QB[:, odd, :, 1, :], QR[:, odd, :, :]).then_inc(s_mid, 1)
                if unit_ok(v):
                    row_max(v, k + 2, 1)
                if not odd and image_ok(n + 1):
                    need(dve, s_v, n + 2)
                    need(dve, s_pv, n * 4)
                    tt_(Va[:, (k // 2 + 1) % 2, :, :, :, 0], PM[:, :].rearrange("p (t h d) -> p t h d", t=TT, h=H),
                        bv_sb[:, :].rearrange("p (o h d) -> p o h d", o=1, h=H).to_broadcast([P, TT, H, D]),
                        ALU.add).then_inc(s_va, 1)
                if odd and image_ok(n - 1):
                    need(dve, s_wp, n)
                    need(dve, s_bp, n * TT)
                    a = hN[:, bass.ds((n - 1) * TT, TT), :]
                    tt_(a, a, PM[:, :].rearrange("p (t e) -> p t e", t=TT), ALU.add).then_inc(s_h2, 1)

            def row_max(v, kv, g):
                b = kv % 2
                need(dve, s_p1, v * 2 + (g + 1))
                need(dve, s_mt, v - 1)
                m = mx[:, b, :].rearrange("p (h t) -> p h t", t=TT)[:, GH * g:GH * (g + 1), :]
                dve.tensor_reduce(m[:, :, 1],
                                  S1[:, 0:1024].rearrange("p (h q) -> p h q", h=GH), AX, ALU.max).then_inc(s_mx, 1)
                dve.tensor_reduce(m[:, :, 0],
                                  S1[:, 1024:1536].rearrange("p (h q) -> p h q", h=GH), AX, ALU.max).then_inc(s_mx, 1)

            dve.wait_ge(s_wts, 16 * 5)
            dve.wait_ge(s_h0, 16 * B * TT)
            slots(dve, slot)

            dve.wait_ge(f_last, 16)
            dve.wait_ge(f_w, 16 * 6)
            dve.bn_stats(lstat[0:B, :], lastr[0:B, :])
            dve.drain()
            dve.bn_aggr(lmv[0:B, :], lstat[0:B, :])
            dve.drain()
            dve.tensor_scalar(lve[0:B, :], lmv[0:B, 1:2], EPS, None, ALU.add).then_inc(f_lst, 1)
            dve.tensor_scalar(bo3, bo3, 0.3, None, ALU.mult)
            dve.wait_ge(f_lrs, 1)
            dve.tensor_scalar(lastr[0:B, :], lastr[0:B, :], lmv[0:B, 0:1], lrstd[0:B, :], ALU.subtract,
                              ALU.mult).then_inc(f_ln, 1)
            dve.wait_ge(f_lt, 1)
            dve.tensor_copy(lastT.rearrange("p (c n) -> p c n", c=CH),
                            PM[:, 0:CH * B].rearrange("p (c n) -> p c n", c=CH)).then_inc(f_lte, 1)
            dve.wait_ge(f_lg, 1)
            tt_(logit[0:B, :], PM[0:B, 0:NX], bp2_sb[0:B, :], ALU.add)
            dve.drain()
            dve.max(top8[0:B, :], logit[0:B, :])
            dve.drain()
            dve.max_index(idx8[:, :], top8[0:B, :], logit[0:B, :]).then_inc(f_idx, 1)

            def ffn_in(n, b):
                ln_stat(n, b, f_stat)
                need(dve, f_base, (n - 1) * TT)
                ln_apply(n, b, f_rstd, f_tr, n - 1, f_xn)

            def ffn_xt(n, b):
                need(dve, f_tr, n + 1)
                need(dve, f_u, (n - 1) * 2)
                dve.tensor_copy(xT[:, b, :, :].rearrange("p c t -> p (c t)"), PM[:, :]).then_inc(f_xt, 1)

            def ffn_out(n, b):
                need(dve, f_d, n + 1)
                need(dve, f_y, n - 1)
                for c in range(CH):
                    bias = WX[b][:, CH * FF + FT * E + FT + c:CH * FF + FT * E + FT + c + 1]
                    dve.tensor_scalar(rT[b][:, c * S:(c + 1) * S], PO[:, c * S:(c + 1) * S], bias, None,
                                      ALU.add).then_inc(f_r, 1)

            def ffn_fin(n, b, m):
                need(dve, f_base, (n + 1) * TT)
                need(dve, f_out[b], m * 16)
                for tt in range(TT):
                    tt_(fin[b][:, tt * E:(tt + 1) * E], h_row(n, tt), bo3, ALU.add)
                dve.drain()
                need(dve, f_y, n + 1)
                for tt in range(TT):
                    f = fin[b][:, tt * E:(tt + 1) * E]
                    dve.scalar_tensor_tensor(out=f, in0=y_ps(b)[:, tt * E:(tt + 1) * E], scalar=0.3, in1=f,
                                             op0=ALU.mult, op1=ALU.add).then_inc(f_fin, 1)

            def ffn(n, b, m):
                ffn_xt(n + 1, 1 - b)
                if not isinstance(n, int) or n + 2 < B:
                    ffn_in(n + 2, b)
                ffn_out(n, b)
                ffn_fin(n, b, m)

            ffn_in(0, 0)
            ffn_in(1, 1)
            ffn_xt(0, 0)
            images(dve, ffn, B - 1)
            ffn_out(B - 1, 1)
            ffn_fin(B - 1, 1, B // 2 - 1)

        @block.tensor
        def _(pe):
            mm = pe.matmul

            pe.wait_ge(s_cst, 18)
            with pe.Fori(0, TILES) as t:
                pe.wait_ge(s_part, t + 1)
                mm(PM[:, 0:10], blkones[:, :], part, start=True, stop=True).then_inc(s_zps, 1)

            def scores_max(v, kv, lap, g):
                r = kv % RING
                if g == 0:
                    need(pe, s_qp[r], (lap + kv // RING + 1) * 96)
                need(pe, s_mx, v * 4 + 2 * g)
                for hh in range(0, GH, 2):
                    dst = S1[:, hh * S:(hh + 2) * S].rearrange("p (h q) -> p h q", h=2)[:, :, P:S]
                    mm(dst, identb[:, :], maskb[:, :].rearrange("p (o k) -> p o k", o=1).to_broadcast([P, 2, P]),
                       start=True, stop=False, skip_group_check=True)
                mm(S1[:, 1024:1536].rearrange("p (h q) -> p h q", h=GH), identb[:, :],
                   maskb[:, :].rearrange("p (o k) -> p o k", o=1).to_broadcast([P, GH, P]),
                   start=True, stop=False, skip_group_check=True)
                for j in range(GH):
                    h = GH * g + j
                    mm(S1[:, j * S:(j + 1) * S], QP[0:KQ, r, h, P:S], KP[0:KQ, r, h, :],
                       start=False, stop=True, skip_group_check=True)
                for j in range(GH):
                    h = GH * g + j
                    ins = mm(S1[:, 1024 + j * P:1024 + (j + 1) * P], QP[0:KQ, r, h, 0:P], KP[0:KQ, r, h, 0:P],
                             start=False, stop=True, skip_group_check=True)
                ins.then_inc(s_p1, 1)

            def scores_exp(u, k, g):
                if g == 0:
                    need(pe, s_mrow, (u + 1) * 32)
                need(pe, s_exp, u * 2 + g)
                for j in range(GH):
                    h = GH * g + j
                    mm(S2[:, j * S:(j + 1) * S], KP[0:KM, k % RING, h, 0:P], QP[0:KM, k % RING, h, :],
                       start=True, stop=True)
                for j in range(GH):
                    h = GH * g + j
                    ins = mm(S2[:, 1024 + j * P:1024 + (j + 1) * P], KP[0:KM, k % RING, h, P:S],
                             QP[0:KM, k % RING, h, P:S], start=True, stop=True)
                ins.then_inc(s_p2, 1)

            def weighted(u, n, k, g):
                if g == 0:
                    need(pe, s_os, u)
                    need(pe, s_va, n + 1)
                need(pe, s_sel, u * 4 + 2 * (g + 1))
                vb = Va[:, (k // 2) % 2, :, :, :, :]
                for kt in range(TT):
                    for j in range(GH):
                        h = (k % 2) * HU + GH * g + j
                        if kt == 0:
                            dst, pr = PO[32 * j:32 * j + 32, g * S:(g + 1) * S], PT[:, g, j * S:(j + 1) * S]
                        else:
                            dst = PO[32 * j:32 * j + 32, g * S + P:(g + 1) * S]
                            pr = PT[:, g, 1024 + j * P:1024 + (j + 1) * P]
                        ins = mm(dst, vb[:, kt, h, :, :].rearrange("p d c -> p (d c)"), pr,
                                 start=(kt == 0), stop=(kt == 1), skip_group_check=True)
                ins.then_inc(s_pv, 1)

            def pm_free(u, n, odd, step, sem_, count):
                if not isinstance(u, int):
                    return need(pe, sem_, count)
                need(pe, s_qa, 2 * min(u + 4 + (step > 0), UNITS))
                need(pe, s_ms, min(u + 1 + (step > 1), UNITS))
                need(pe, s_va, min(n + 1 + (odd or step > 2), B))
                need(pe, s_h2, min(n - 1 + (odd and step > 2), B))
                need(pe, s_xt, min(n + 3, B))

            def slot(u, n, k, lap):
                v, w, odd = u + 2, u + 4, k % 2
                if unit_ok(u):
                    scores_exp(u, k, 0)
                if unit_ok(w):
                    if odd:
                        pm_free(u, n, odd, 0, s_va, n + 2)
                    else:
                        pm_free(u, n, odd, 0, s_xt, n + 3)
                    for o in range(2):
                        for c in range(CH):
                            ins = mm(PM[:, o * S:(o + 1) * S], w1_sb[:, c, o, odd * P:(odd + 1) * P],
                                     xT[:, (k // 2) % 2, c, :], start=(c == 0), stop=(c == CH - 1))
                    ins.then_inc(s_d, 1)
                if unit_ok(v):
                    scores_max(v, k + 2, lap, 0)
                if unit_ok(u):
                    scores_exp(u, k, 1)
                if unit_ok(u + 1):
                    pm_free(u, n, odd, 1, s_qa, (u + 5) * 2)
                    need(pe, s_mx, (u + 2) * 4)
                    pe.transpose(PM[0:TT * HU, 0:P], mx[:, (k + 1) % 2, :], ident[:, :]).then_inc(s_mt, 1)
                if unit_ok(u):
                    weighted(u, n, k, 0)
                if unit_ok(v):
                    scores_max(v, k + 2, lap, 1)
                if not odd and image_ok(n + 1):
                    pm_free(u, n, odd, 2, s_ms, u + 2)
                    for tt in range(TT):
                        for c in range(CH):
                            ins = mm(PM[:, tt * E:(tt + 1) * E], xT[:, (k // 2 + 1) % 2, c, tt * P:(tt + 1) * P],
                                     w1_sb[:, c, 2, :], start=(c == 0), stop=(c == CH - 1))
                    ins.then_inc(s_v, 1)
                if odd and image_ok(n - 1):
                    pm_free(u, n, odd, 2, s_ms, u + 2)
                    need(pe, s_ac, n * 2)
                    for tt in range(TT):
                        for c in range(UPI):
                            ins = mm(PM[:, tt * E:(tt + 1) * E],
                                     AC[:, ((k // 2 - 1) * 2 + c) % RING, tt * P:(tt + 1) * P],
                                     wp_sb[:, c, :], start=(c == 0), stop=(c == UPI - 1))
                    ins.then_inc(s_wp, 1)
                if unit_ok(u):
                    weighted(u, n, k, 1)
                if odd and image_ok(n + 3):
                    pm_free(u, n, odd, 3, s_h2, n)
                    need(pe, s_xn, (n + 4) * TT)
                    for c in range(CH):
                        for tt in range(TT):
                            ins = pe.transpose(PM[:, c * S + tt * P:c * S + (tt + 1) * P],
                                               xn[:, (k // 2 + 3) % 2, tt, c * P:(c + 1) * P], ident[:, :])
                    ins.then_inc(s_tr, 1)

            pe.wait_ge(s_wts, 16 * 5)
            slots(pe, slot)

            pe.wait_ge(f_ln, 1)
            pe.wait_ge(s_h2, B)
            for c in range(CH):
                ins = pe.transpose(PM[:, c * B:(c + 1) * B], lastr[0:B, c * P:(c + 1) * P], ident[0:B, 0:B])
            ins.then_inc(f_lt, 1)
            pe.wait_ge(f_lte, 1)
            pe.wait_ge(f_w, 16 * 6)
            for c in range(CH):
                ins = mm(PM[:, 0:B], wp1_sb[:, c * NAV:(c + 1) * NAV], lastT[:, c * B:(c + 1) * B],
                         start=(c == 0), stop=(c == CH - 1))
            ins.then_inc(f_ga, 1)
            pe.wait_ge(f_gae, 1)
            mm(PM[0:B, 0:NX], gact, wp2_sb, start=True, stop=True).then_inc(f_lg, 1)
            pe.wait_ge(f_idx, 1)

            def ffn_tr(n, b):
                need(pe, f_xn, (n + 1) * TT)
                need(pe, f_xt, n)
                for c in range(CH):
                    for tt in range(TT):
                        ins = pe.transpose(PM[:, c * S + tt * P:c * S + (tt + 1) * P], xn[:, b, tt, c * P:(c + 1) * P],
                                           ident[:, :])
                ins.then_inc(f_tr, 1)

            def ffn_up(n, b, m):
                need(pe, f_xt, n + 1)
                pe.wait_ge(f_wx[b], (m + 1) * 16)
                need(pe, f_g, (n - 1) * FT)
                for f in range(FT):
                    for c in range(CH):
                        ins = mm((S1 if b == 0 else S2)[:, f * S:(f + 1) * S],
                                 WX[b][:, c * FF + f * P:c * FF + (f + 1) * P], xT[:, b, c, :],
                                 start=(c == 0), stop=(c == CH - 1))
                    if f % 2:
                        ins.then_inc(f_u, 1)

            def ffn_down(n, b):
                need(pe, f_g, (n + 1) * FT)
                need(pe, f_r, n * CH)
                for c in range(CH):
                    for f in range(FT):
                        w0 = CH * FF + f * E + c * P
                        ins = mm(PO[:, c * S:(c + 1) * S], WX[b][:, w0:w0 + P], gT[b][:, f * S:(f + 1) * S],
                                 start=(f == 0), stop=(f == FT - 1))
                ins.then_inc(f_d, 1)

            def ffn_y(n, b):
                need(pe, f_r, (n + 1) * CH)
                need(pe, f_fin, (n - 1) * TT)
                for tt in range(TT):
                    for c in range(CH):
                        ins = mm(y_ps(b)[:, tt * E:(tt + 1) * E], rT[b][:, c * S + tt * P:c * S + (tt + 1) * P],
                                 wo_sb[:, c * E:(c + 1) * E], start=(c == 0), stop=(c == CH - 1))
                ins.then_inc(f_y, 1)

            def ffn(n, b, m):
                ffn_tr(n + 1, 1 - b)
                ffn_down(n, b)
                ffn_up(n + 1, 1 - b, m + b)
                ffn_y(n, b)

            ffn_tr(0, 0)
            ffn_up(0, 0, 0)
            images(pe, ffn, B - 1)
            ffn_down(B - 1, 1)
            ffn_y(B - 1, 1)


def layouts(a):
    c = np.ascontiguousarray
    img = a["x"].reshape(TILES, P, 8 * E)
    fine = []
    for name, (r, w) in zip(("L0_tok_Wd3", "L0_tok_Wd2", "L0_tok_Wd1"), LVL):
        fine.append(a[name].reshape(3, BLK, r, w, 3).transpose(1, 4, 0, 2, 3).reshape(BLK, -1))
    wd = np.concatenate(fine + [a["L0_tok_Wa"].reshape(BLK, -1)], axis=1)
    bd = np.concatenate([a["L0_tok_bd3"], a["L0_tok_bd2"], a["L0_tok_bd1"], a["L0_tok_ba"]]).reshape(1, 10)
    w1 = a["L0_attn_W1"].reshape(CH, P, H, 3, D)
    qk = w1[:, :, :, 0:2].reshape(CH, P, UPI, HU, 2, D).transpose(1, 0, 4, 2, 5, 3).reshape(P, CH, 2, E)
    v = w1[:, :, :, 2].transpose(1, 0, 2, 3).reshape(P, CH, 1, E)
    b1 = a["L0_attn_b1"].reshape(H, 3, D)
    bqk = b1[:, 0:2].reshape(UPI, HU, 2, D).transpose(3, 1, 0, 2).reshape(P, UPI, 2)
    wp = a["L0_attn_Wp"].reshape(UPI, 2, GH, D, E).transpose(2, 3, 1, 0, 4).reshape(P, UPI, E)
    wx = np.concatenate([
        a["L0_ffn_W1"].reshape(NX, CH, P, FF).transpose(0, 2, 1, 3).reshape(NX, P, -1),
        a["L0_ffn_W2"].reshape(NX, FT, P, E).transpose(0, 2, 1, 3).reshape(NX, P, -1),
        a["L0_ffn_b1"].reshape(NX, FT, P).transpose(0, 2, 1),
        a["L0_ffn_b2"].reshape(NX, CH, P).transpose(0, 2, 1)], axis=2)
    rows = lambda m: m.reshape(-1, P, m.shape[1]).transpose(1, 0, 2).reshape(P, -1)
    return {
        "x": c(img), "wd": c(wd), "bd": c(bd), "w1": c(np.concatenate([qk, v], axis=2)), "bqk": c(bqk),
        "bv": c(b1[:, 2].reshape(1, E)), "wp": c(wp), "bp": c(a["L0_attn_bp"].reshape(1, E)),
        "wp1": c(rows(a["L0_ffn_Wp1"])), "bp1": c(a["L0_ffn_bp1"].reshape(P, 1)), "wp2": c(a["L0_ffn_Wp2"]),
        "bp2": c(a["L0_ffn_bp2"].reshape(1, NX)), "wx": c(wx), "wo": c(rows(a["L0_ffn_Wo"])),
        "bo": c(a["L0_ffn_bo"].reshape(1, E)),
    }


def kernel(**inputs):
    import concourse.bacc as bacc
    from concourse.bass_utils import run_bass_kernel_spmd

    nc = bacc.Bacc("TRN2", target_bir_lowering=False, num_devices=1)
    arrays = layouts({k: np.asarray(v) for k, v in inputs.items()})
    args = {k: nc.dram_tensor(f"in_{k}", v.shape, mybir.dt.from_np(v.dtype), kind="ExternalInput").ap()
            for k, v in arrays.items()}
    args["out"] = nc.dram_tensor("out_h", (B, S, E), F32, kind="ExternalOutput").ap()
    tower(nc, **args)
    r = run_bass_kernel_spmd(nc, [{f"in_{k}": v for k, v in arrays.items()}], core_ids=[0])
    return r.results[0]["out_h"]
```

```python
from contextlib import ExitStack

import numpy as np

import concourse.bass as bass
from concourse import mybir

F32 = mybir.dt.float32
F32R = mybir.dt.float32r
BF16 = mybir.dt.bfloat16
U32 = mybir.dt.uint32
ALU = mybir.AluOpType
ACT = mybir.ActivationFunctionType
AX = mybir.AxisListType.X

P = 128
B, S, E = 16, 256, 256
H, D = 16, 16
NX, FF, NAV = 8, 512, 128
TT, CH, FT = S // P, E // P, FF // P
EPS = 1e-5
BLK = S // 8
IPT = P // BLK
TILES = B // IPT
UPI = 2
HU = H // UPI
UNITS = B * UPI
GH = 4
SLOTS = 6
KQ = SLOTS * D
KM = KQ + 2
RING = 4
BIG = -1.0e6
LVL = ((4, 128), (2, 64), (1, 32))
LW = [3 * r * c for r, c in LVL]
WD_OFF = [0, 3 * LW[0], 3 * (LW[0] + LW[1]), 3 * sum(LW)]
CONSTANTS = 12 + IPT
WD_W = 3 * sum(LW) + LVL[2][0] * LVL[2][1]
ARENA = 16960
WX_W = CH * FF + FT * E + FT + CH


def tower(nc, x, wd, bd, w1, bqk, bv, wp, bp, wp1, bp1, wp2, bp2, wx, wo, bo, out):
    bounce = nc.dram_tensor("bounce", [RING, 2, 3, P, S], BF16).ap()
    with ExitStack() as ctx:
        def sb(name, shape, dt=F32):
            return ctx.enter_context(nc.sbuf_tensor(name, shape, dt))

        def sem(name):
            return ctx.enter_context(nc.semaphore(name))

        S1 = ctx.enter_context(nc.psum_tensor("S1", [P, 1536], F32))
        S2 = ctx.enter_context(nc.psum_tensor("S2", [P, 1536], F32))
        PO = ctx.enter_context(nc.psum_tensor("PO", [P, 512], F32))
        PM = ctx.enter_context(nc.psum_tensor("PM", [P, 512], F32))

        hN = sb("hN", [P, B * TT, E])
        ident = sb("ident", [P, P])
        identb = sb("identb", [P, P], BF16)
        maskb = sb("maskb", [P, P], BF16)
        blkones = sb("blkones", [P, P])
        half = sb("half", [P, 2])
        stat = sb("stat", [P, 2, TT, 6])
        mv = sb("mv", [P, 2, TT, 2])
        ve = sb("ve", [P, 2, TT])
        rstd = sb("rstd", [P, 2, TT])
        xn = sb("xn", [P, 2, TT, E])
        xTH = sb("xTH", [P, 2, CH, S], F32R)
        xTL = sb("xTL", [P, 2, CH, S], F32R)
        idx8 = sb("idx8", [B // 2, 2, 8], U32)
        idxr = sb("idxr", [1, B], U32)

        mB = sb("mB", [TT * HU, 2, 2, P], BF16)

        early = ExitStack()

        def sb(name, shape, dt=F32):
            return early.enter_context(nc.sbuf_tensor(name, shape, dt))

        QP = sb("QP", [P, RING, HU, S], BF16)
        KP = sb("KP", [P, RING, HU, S], BF16)
        arena = sb("arena", [P, ARENA])
        cur = [0]

        def carve(n):
            a = arena[:, cur[0]:cur[0] + n]
            cur[0] += n
            return a

        w1H = sb("w1H", [P, CH, 3, E], F32R)
        w1L = sb("w1L", [P, CH, 3, E], F32R)
        w1_sb = QP[:, :, :, :].rearrange("p r h t -> p (r h t)")[:, 0:2 * CH * 3 * E].bitcast(F32).rearrange(
            "p (c o e) -> p c o e", c=CH, o=3)
        wp_sb = sb("wp_sb", [P, UPI, E])
        bqk_sb = sb("bqk_sb", [P, UPI, 2])
        bv_sb = sb("bv_sb", [P, E])
        bp_sb = sb("bp_sb", [P, E])
        QF = sb("QF", [P, 2, 2, S])
        QR = sb("QR", [P, 2, 2, S])
        QB = sb("QB", [P, 2, 2, 3, S], BF16)
        Va = sb("Va", [P, 2, TT, H, D, 2])
        PT = sb("PT", [P, 2, 1536])
        OS = sb("OS", [P, 2, 2, S])
        AU = sb("AU", [P, 2, S])
        SC = sb("SC", [P, 2, S])
        AC = sb("AC", [P, RING, S])
        mx = sb("mx", [P, 2, TT * HU])

        cur[0] = 0
        flat4 = lambda m: m[:, :, :, :].rearrange("p a b c -> p (a b c)")
        X = carve(8 * E)
        ALO = [flat4(QF)] + [carve(2 * r * c) for r, c in LVL[1:]]
        AHI = [flat4(QR)] + [carve(2 * r * c) for r, c in LVL[1:]]
        SLO = [AC[:, :, :].rearrange("p a b -> p (a b)")] + [carve(2 * r * c) for r, c in LVL[1:]]
        SHI = [flat4(OS)] + [carve(2 * r * c) for r, c in LVL[1:]]
        DT = [carve(n) for n in LW]
        GT = [carve(n) for n in LW]
        AA = [carve(r * c) for r, c in LVL]
        GA = [carve(r * c) for r, c in LVL]
        RX = carve(8 * E)
        WD = carve(WD_W)
        part = carve(10)
        z = carve(10)
        ez = carve(10)
        es = carve(10)
        zmax = carve(3)
        zsum = carve(4)
        zrec = carve(4)
        wg = carve(10)
        bdt = carve(10)
        wscale = carve(10)
        assert cur[0] <= ARENA

        early.close()

        def late(name, n, dt=F32R):
            return [ctx.enter_context(nc.sbuf_tensor(f"{name}{b}", [P, n], dt))[:, :] for b in range(2)]

        wH = late("wH", CH * FF + FT * E)
        wL = late("wL", CH * FF + FT * E)
        gH, gL = late("gH", FT * S), late("gL", FT * S)
        rH, rL = late("rH", CH * S), late("rL", CH * S)
        xH, xL = ([m[:, b, :, :].rearrange("p c t -> p (c t)") for b in range(2)] for m in (xTH, xTL))
        woH, woL = late("wo_parts", CH * E)
        W1_, W2_ = slice(0, CH * FF), slice(CH * FF, CH * FF + FT * E)
        FARENA = ARENA - 2 * (2 * FT * S + 2 * CH * S) - 2 * CH * E
        farena = ctx.enter_context(nc.sbuf_tensor("farena", [P, FARENA], F32))
        cur[0] = 0

        def carve(n):
            a = farena[:, cur[0]:cur[0] + n]
            cur[0] += n
            return a

        WX = [carve(WX_W) for _ in range(2)]
        WB = [carve(FT + CH) for _ in range(2)]
        gT = [carve(FT * S) for _ in range(2)]
        fin = [carve(TT * E) for _ in range(2)]
        wo_sb = carve(CH * E)
        bo3 = carve(E)
        wp1_sb = carve(CH * NAV)
        wp2_sb = carve(NX)
        bp1_sb = carve(1)
        bp2_sb = carve(NX)
        lastr = carve(E)
        lstat = carve(6)
        lmv = carve(2)
        lve = carve(1)
        lrstd = carve(1)
        lastT = carve(CH * B)
        gact = carve(B)
        logit = carve(NX)
        top8 = carve(NX)
        assert cur[0] <= FARENA

        s_cst = sem("s_cst")
        s_ones = sem("s_ones")
        s_x = sem("s_x")
        s_wdc = sem("s_wdc")
        s_wd = sem("s_wd")
        s_wts = sem("s_wts")
        s_xfree = sem("s_xfree")
        s_dhi = sem("s_dhi")
        s_prod = sem("s_prod")
        s_psum = sem("s_psum")
        s_slo = sem("s_slo")
        s_shi = sem("s_shi")
        s_part = sem("s_part")
        s_zps = sem("s_zps")
        s_z = sem("s_z")
        s_ez = sem("s_ez")
        s_wg = sem("s_wg")
        s_gate = sem("s_gate")
        s_recd = sem("s_recd")
        s_recp = sem("s_recp")
        s_h0 = sem("s_h0")
        s_stat = sem("s_stat")
        s_rstd = sem("s_rstd")
        s_xn = sem("s_xn")
        s_bp = sem("s_bp")
        s_tr = sem("s_tr")
        s_xh = sem("s_xh")
        s_xt = sem("s_xt")
        s_w1 = sem("s_w1")
        s_d = sem("s_d")
        s_qa = sem("s_qa")
        s_hi = sem("s_hi")
        s_r1 = sem("s_r1")
        s_mid = sem("s_mid")
        s_lo = sem("s_lo")
        s_scr = sem("s_scr")
        s_qp = [sem(f"s_qp{r}") for r in range(RING)]
        s_p1 = sem("s_p1")
        s_mx = sem("s_mx")
        s_mt = sem("s_mt")
        s_ms = sem("s_ms")
        s_mrow = sem("s_mrow")
        s_p2 = sem("s_p2")
        s_exp = sem("s_exp")
        s_sel = sem("s_sel")
        s_pv = sem("s_pv")
        s_os = sem("s_os")
        s_oc = [sem(f"s_oc{b}") for b in range(2)]
        s_ac = sem("s_ac")
        s_v = sem("s_v")
        s_va = sem("s_va")
        s_wp = sem("s_wp")
        s_h2 = sem("s_h2")
        s_turn = sem("s_turn")
        act_turn = sem("act_turn")
        sp_turn = sem("sp_turn")
        f_w = sem("f_w")
        f_last = sem("f_last")
        f_lst = sem("f_lst")
        f_lrs = sem("f_lrs")
        f_ln = sem("f_ln")
        f_lt = sem("f_lt")
        f_lte = sem("f_lte")
        f_ga = sem("f_ga")
        f_gae = sem("f_gae")
        f_lg = sem("f_lg")
        f_lge = sem("f_lge")
        f_idx = sem("f_idx")
        f_idr = sem("f_idr")
        f_wx1 = [sem(f"f_wx1{b}") for b in range(2)]
        f_wx2 = [sem(f"f_wx2{b}") for b in range(2)]
        f_rh = sem("f_rh")
        f_stat = sem("f_stat")
        f_rstd = sem("f_rstd")
        f_xn = sem("f_xn")
        f_base = sem("f_base")
        f_tr = sem("f_tr")
        f_xh = sem("f_xh")
        f_xt = sem("f_xt")
        f_wb = sem("f_wb")
        f_h1 = sem("f_h1")
        f_l1 = sem("f_l1")
        f_h2 = sem("f_h2")
        f_l2 = sem("f_l2")
        f_ge = sem("f_ge")
        f_gh = sem("f_gh")
        f_wo = sem("f_wo")
        f_u = sem("f_u")
        f_g = sem("f_g")
        f_d = sem("f_d")
        f_r = sem("f_r")
        f_y = sem("f_y")
        f_fin = sem("f_fin")
        f_out = [sem(f"f_out{b}") for b in range(2)]

        def need(eng, s, v):
            if not isinstance(v, int) or v > 0:
                eng.wait_ge(s, v)

        def h_row(n, tt):
            return hN[:, bass.ds(n * TT + tt, 1), :].rearrange("p o e -> p (o e)")

        def bcast(ap, shape):
            return ap.to_broadcast(shape)

        FIRST, LAST = -3 * UPI, UNITS + 1
        LOOP0, LOOPS = 4, 5
        ROUTE0 = LOOP0 + 4 * LOOPS
        NR = B // 2

        def slots(eng, body, router):
            for u in range(FIRST + 3, LOOP0):
                body(u, u // 2, u, 0)
            with eng.Fori(0, LOOPS) as it:
                for k in range(4):
                    body(it * 4 + (LOOP0 + k), it * 2 + (LOOP0 + k) // 2, k, it + LOOP0 // RING)
            for u in range(ROUTE0, UNITS - 1):
                body(u, u // 2, u, 0)
                router(0, u - ROUTE0)

        def last_slot(body, u):
            body(u, u // 2, u, 0)

        def images(eng, body, count, done=0):
            turns = (B - 2) // 2
            for n in range(done, 2):
                body(n, n, 0)
            with eng.Fori(max(done // 2, 1), turns) as it:
                for b in range(2):
                    body(it * 2 + b, b, it)
            for n in range(turns * 2, count):
                body(n, n % 2, n // 2)

        def nothing(t):
            pass

        def tiles(eng, gates, synthesis, slot, split=nothing):
            def first(i):
                slot(FIRST + i, (FIRST + i) // 2, FIRST + i, 0)

            gates(0)
            synthesis(0)
            with eng.Fori(1, TILES - 1) as t:
                gates(t)
                synthesis(t)
            eng.wait_ge(s_wts, 16 * 5)
            eng.wait_ge(s_ones, 3)
            first(0)
            first(1)
            split(TILES)
            gates(TILES - 1)
            first(2)
            synthesis(TILES - 1)


        def first_tile(t):
            return isinstance(t, int) and t == 0

        def last_tile(t):
            return isinstance(t, int) and t == TILES - 1

        fr, fc = LVL[0]
        VROWS = 5
        x3 = X.rearrange("p (r c) -> p r c", r=2 * fr)
        rx3 = RX.rearrange("p (r c) -> p r c", r=2 * fr)
        alo3, ahi3, slo3, shi3 = (m.rearrange("p (r c) -> p r c", r=2 * fr) for m in (ALO[0], AHI[0], SLO[0], SHI[0]))
        d4, g4 = (m.rearrange("p (k r c) -> p k r c", k=3, r=fr) for m in (DT[0], GT[0]))

        def rows_out(eng, need_eng, t):
            need_eng(s_recd, t + 1)
            need_eng(s_recp, t + 1)
            for i in range(IPT):
                for tt in range(TT):
                    p0 = BLK * i + BLK // TT * tt
                    eng.dma_start(h_row(t * IPT + i, tt),
                                  RX[p0:p0 + BLK // TT, :].rearrange("p (r e) -> p r e", r=8)).then_inc(s_h0, 16)

        def columns_merged(eng, r0, r1):
            lo, hi = slo3[:, r0:r1, :], shi3[:, r0:r1, :]
            eng.tensor_tensor(rx3[:, r0:r1, 0::2], lo, hi, ALU.add)
            return eng.tensor_tensor(rx3[:, r0:r1, 1::2], lo, hi, ALU.subtract)

        def unit_ok(u):
            return not isinstance(u, int) or 0 <= u < UNITS

        def image_ok(n):
            return not isinstance(n, int) or 0 <= n < B

        def y_ps(b):
            return (S1 if b == 0 else S2)[:, 1024:1536]

        block = ctx.enter_context(nc.Block())

        @block.gpsimd
        def _(pool):
            pool.memset(ident[:, :], 0.0).then_inc(s_cst, 1)
            pool.memset(identb[:, :], 0.0).then_inc(s_cst, 1)
            pool.memset(maskb[:, :], 0.0).then_inc(s_cst, 1)
            pool.memset(blkones[:, :], 0.0).then_inc(s_cst, 1)
            pool.memset(half[:, :], -0.5).then_inc(s_cst, 1)
            for l in range(3):
                pool.memset(wscale[:, 3 * l:3 * l + 3], 0.25 ** (l + 1)).then_inc(s_cst, 1)
            pool.memset(wscale[:, 9:10], 0.25 ** 3).then_inc(s_cst, 1)
            pool.wait_ge(s_cst, 9)
            for m in (ident, identb):
                pool.affine_select(out=m[:, :], in_=m[:, :], compare_op=ALU.not_equal, fill=1.0, base=0,
                                   pattern=[[-1, P]], channel_multiplier=1).then_inc(s_cst, 1)
            pool.affine_select(out=maskb[:, :], in_=maskb[:, :], compare_op=ALU.is_ge, fill=BIG, base=0,
                               pattern=[[-1, P]], channel_multiplier=1).then_inc(s_cst, 1)
            for i in range(IPT):
                pool.wait_ge(s_cst, 12 + i)
                pool.memset(blkones[BLK * i:BLK * i + BLK, BLK * i:BLK * i + BLK], 1.0).then_inc(s_cst, 1)

            def slot(u, n, k, lap):
                w, odd = u + 4, k % 2
                if unit_ok(u):
                    select(u, 0)
                if unit_ok(w):
                    need(pool, s_hi, w + 1)
                    need(pool, s_lo, w - 1)
                    pool.tensor_tensor(QR[:, odd, :, :], QF[:, odd, :, :], QB[:, odd, :, 0, :],
                                       ALU.subtract).then_inc(s_r1, 1)
                if unit_ok(u):
                    select(u, 1)
                if unit_ok(w):
                    need(pool, s_mid, w + 1)
                    pool.tensor_tensor(QB[:, odd, :, 2, :], QR[:, odd, :, :], QB[:, odd, :, 1, :],
                                       ALU.subtract).then_inc(s_lo, 1)
                if not odd and image_ok(n + 3):
                    b = (k // 2 + 3) % 2
                    need(pool, s_stat, n + 4)
                    pool.tensor_tensor(rstd[:, b, :], ve[:, b, :], half[:, :], ALU.pow).then_inc(s_rstd, 1)
                if odd and image_ok(n + 3):
                    need(pool, s_xn, (n + 4) * TT)
                    for tt in range(TT):
                        a = h_row(n + 3, tt)
                        pool.tensor_tensor(a, a, bp_sb[:, :], ALU.add).then_inc(s_bp, 1)

            def select(u, g):
                need(pool, s_exp, u * 2 + (g + 1))
                pool.sem_inc(s_turn, 1)
                pt = PT[:, g, :]
                for v in (pt[:, 0:1024].rearrange("p (h q) -> p h q", h=GH)[:, :, 0:P],
                          pt[:, 1024:1536].rearrange("p (h q) -> p h q", h=GH)):
                    pool.affine_select(out=v, in_=v, compare_op=ALU.is_ge, fill=0.0, base=0,
                                       pattern=[[0, GH], [1, P]], channel_multiplier=-1).then_inc(s_sel, 1)

            def high_columns(t):
                need(pool, s_x, (t + 1) * 16)
                pool.tensor_tensor(ahi3, x3[:, :, 0::2], x3[:, :, 1::2], ALU.subtract).then_inc(s_xfree, 1)

            def high_details(t):
                if not first_tile(t):
                    need(pool, s_gate, t * 10)
                need(pool, s_xfree, (t + 1) * 2)
                pool.tensor_tensor(d4[:, 1], ahi3[:, 0::2, :], ahi3[:, 1::2, :], ALU.add).then_inc(s_dhi, 1)
                pool.tensor_tensor(d4[:, 2], ahi3[:, 0::2, :], ahi3[:, 1::2, :], ALU.subtract).then_inc(s_dhi, 1)

            def tile_gates(t):
                need(pool, s_part, t * 4 + 1)
                need(pool, s_dhi, (t + 1) * 2)
                w0 = WD_OFF[0] + 2 * LW[0]
                pool.tensor_tensor(PT[:, 1, 0:LW[0]], DT[0], WD[:, w0:w0 + LW[0]], ALU.mult).then_inc(s_prod, 1)

            def tile_synthesis(t):
                if not last_tile(t):
                    high_columns(t + 1)
                need(pool, s_gate, t * 10 + 9)
                pool.tensor_tensor(shi3[:, 0::2, :], g4[:, 1], g4[:, 2], ALU.add).then_inc(s_shi, 1)
                pool.tensor_tensor(shi3[:, 1::2, :], g4[:, 1], g4[:, 2], ALU.subtract).then_inc(s_shi, 1)
                need(pool, s_slo, t + 1)
                need(pool, s_shi, (t + 1) * 2)
                if not first_tile(t):
                    need(pool, s_h0, t * (16 * IPT * TT))
                columns_merged(pool, VROWS, 2 * fr).then_inc(s_recp, 1)
                if not last_tile(t):
                    high_details(t + 1)

            pool.wait_ge(s_cst, CONSTANTS)
            pool.memset(KP[KQ:P, 0:2, :, :], 1.0).then_inc(s_ones, 1)
            pool.wait_ge(s_ones, 1)
            high_columns(0)
            high_details(0)
            pool.wait_ge(s_dhi, 2)
            pool.memset(KP[KQ:P, 2:RING, :, :], 1.0).then_inc(s_ones, 1)
            pool.wait_ge(s_ones, 2)
            pool.memset(Va[:, :, :, :, :, 1], 1.0).then_inc(s_ones, 1)
            pool.wait_ge(s_wd, 16 * (IPT + 1))
            def split_w1(t):
                pool.wait_ge(s_w1, 1)
                pool.tensor_tensor(w1L[:, :, :, :], w1_sb, w1H[:, :, :, :], ALU.subtract).then_inc(s_w1, 1)

            tiles(pool, tile_gates, tile_synthesis, slot, split_w1)
            def router(part_, step):
                if step == 1:
                    need(pool, f_lst, part_ + 1)
                    pool.tensor_tensor(lrstd[0:NR, :], lve[0:NR, :], half[0:NR, 0:1], ALU.pow).then_inc(f_lrs, 1)

            def split_1(n, b):
                need(pool, f_h1, n + 1)
                pool.tensor_tensor(wL[b][:, W1_], WX[b][:, W1_], wH[b][:, W1_], ALU.subtract).then_inc(f_l1, 1)

            def split_2(n, b):
                need(pool, f_h2, n + 1)
                pool.tensor_tensor(wL[b][:, W2_], WX[b][:, W2_], wH[b][:, W2_], ALU.subtract).then_inc(f_l2, 1)

            def deviation(n, b):
                need(pool, f_stat, n + 1)
                pool.tensor_tensor(rstd[:, b, :], ve[:, b, :], half[:, :], ALU.pow).then_inc(f_rstd, 1)

            def residual(n, b):
                need(pool, f_xn, (n + 1) * TT)
                for tt in range(TT):
                    a = h_row(n, tt)
                    pool.tensor_tensor(a, a, xn[:, b, tt, :], ALU.add).then_inc(f_base, 1)

            def ffn(n, b, m):
                if not isinstance(n, int) or n + 2 < B:
                    deviation(n + 2, b)
                split_2(n + 1, 1 - b)
                if not isinstance(n, int) or n + 2 < B:
                    split_1(n + 2, b)
                    residual(n + 2, b)

            slots(pool, slot, router)
            deviation(0, 0)
            split_1(0, 0)
            deviation(1, 1)
            last_slot(slot, UNITS - 1)
            split_2(0, 0)
            split_1(1, 1)
            residual(0, 0)
            residual(1, 1)
            ffn(0, 0, 0)
            deviation(3, 1)
            residual(3, 1)
            pool.wait_ge(f_base, 4 * TT)
            router(1, 1)
            pool.wait_ge(f_lrs, 2)
            split_2(2, 0)
            split_1(3, 1)
            for n in range(2, 4):
                ffn(n, n % 2, 1)
            images(pool, ffn, B - 1, done=4)

        @block.sync
        def _(sp):
            def need_sp(s, v):
                need(sp, s, v)
                if not isinstance(v, int):
                    sp.sem_inc(sp_turn, 1)

            sp.dma_start(X, x[0]).then_inc(s_x, 16)
            for part_, c0, c1 in ((s_wdc, WD_OFF[1], WD_W), (s_wd, 0, WD_OFF[1])):
                for i in range(IPT):
                    sp.dma_start(WD[BLK * i:BLK * i + BLK, c0:c1], wd[:, c0:c1]).then_inc(part_, 16)
            sp.dma_start(bdt, bcast(bd, [P, 10])).then_inc(s_wd, 16)
            sp.wait_ge(s_xfree, 2)
            sp.dma_start(X, x[1]).then_inc(s_x, 16)
            sp.dma_start(w1_sb, w1).then_inc(s_wts, 16)
            sp.dma_start(wp_sb[:, :, :], wp).then_inc(s_wts, 16)
            sp.dma_start(bqk_sb[:, :, :], bqk).then_inc(s_wts, 16)
            sp.dma_start(bv_sb[:, :], bcast(bv, [P, E])).then_inc(s_wts, 16)
            sp.dma_start(bp_sb[:, :], bcast(bp, [P, E])).then_inc(s_wts, 16)

            def tile(t):
                if not first_tile(t) and not last_tile(t):
                    need_sp(s_xfree, (t + 1) * 2)
                    src = x[t + 1] if isinstance(t, int) else x[bass.ds(t + 1, 1)].rearrange("o p c -> (o p) c")
                    sp.dma_start(X, src).then_inc(s_x, 16)

            def slot(u, n, k, lap):
                w = u + 3
                if unit_ok(u - 1):
                    b = (k - 1) % 2
                    need_sp(s_os, u)
                    need_sp(s_ac, u - 2)
                    for c, dst in ((0, AU), (1, SC)):
                        sp.dma_start(dst[:, b, :], OS[c:P:2, b, :, :]).then_inc(s_oc[b], 16)
                if unit_ok(w):
                    r = (k + 3) % RING
                    need_sp(s_scr, (w + 1) * 16)
                    need_sp(s_p2, (w - 3) * 2)
                    for o, dst, plan in ((0, QP, ((0, 0, 3, 3), (3, 0, 2, 2), (5, 0, 1, 1))),
                                         (1, KP, ((0, 0, 1, 3), (3, 1, 1, 2), (5, 2, 1, 1)))):
                        for at, part0, parts, count in plan:
                            src = bounce[r, o, part0:part0 + parts].rearrange("s (d h) t -> (s d) (h t)", h=HU)
                            if parts < count:
                                src = bounce[r, o, part0:part0 + 1].rearrange(
                                    "s (d h) t -> s d (h t)", h=HU).to_broadcast([count, D, HU * S])
                            sp.dma_start(dst[at * D:(at + count) * D, r, :, :], src).then_inc(s_qp[r], 16)
                if isinstance(u, int) and u == -1:
                    rows_out(sp, need_sp, TILES - 1)
                w = u + 4
                if unit_ok(w):
                    need_sp(s_lo, w + 1)
                    need_sp(s_qp[k % RING], (lap + (k + 4) // RING) * 96)
                    sp.dma_start(bounce[k % RING].rearrange("o s p t -> p (o s) t"),
                                 QB[:, k % 2, :, :, :].rearrange("p o s t -> p (o s) t")).then_inc(s_scr, 16)

            tiles(sp, tile, nothing, slot)
            def router(part_, step):
                if step == 0:
                    if part_ == 0:
                        sp.wait_ge(s_h0, 16 * B * TT)
                        sp.dma_start(wo_sb, wo).then_inc(f_w, 16)
                        sp.dma_start(bo3, bcast(bo, [P, E])).then_inc(f_w, 16)
                        sp.dma_start(wp1_sb, wp1).then_inc(f_w, 16)
                        sp.dma_start(wp2_sb, wp2).then_inc(f_w, 16)
                        sp.dma_start(bp1_sb, bp1).then_inc(f_w, 16)
                        sp.dma_start(bp2_sb[0:NR, :], bcast(bp2, [NR, NX])).then_inc(f_w, 16)
                    sp.wait_ge(s_h2, (part_ + 1) * NR)
                    i0 = part_ * NR * TT
                    sp.dma_start(lastr[0:NR, :], hN[P - 1:P, i0 + 1:i0 + NR * TT:TT, :]).then_inc(f_last, 16)
                if step == 5:
                    sp.wait_ge(f_idx, part_ + 1)
                    sp.dma_start(idxr[:, part_ * NR:(part_ + 1) * NR], idx8[:, part_, 0:1]).then_inc(f_idr, 16)
                    sp.wait_ge(f_idr, 16 * (part_ + 1))
                    if part_ == 0:
                        for n in range(2):
                            load_expert(n, n)

            def load_expert(n, b):
                e = sp.value_load(idxr[0:1, bass.ds(n, 1)], min_val=0, max_val=NX - 1)
                src = wx[bass.ds(e, 1)].rearrange("o p c -> (o p) c")
                need_sp(f_l1, n - 1)
                sp.dma_start(WX[b][:, W1_], src[:, W1_]).then_inc(f_wx1[b], 16)
                need_sp(f_l2, n - 1)
                need_sp(f_wb, n - 1)
                sp.dma_start(WX[b][:, CH * FF:WX_W], src[:, CH * FF:WX_W]).then_inc(f_wx2[b], 16)

            def store(n, b):
                need_sp(f_fin, (n + 1) * TT)
                sp.dma_start(out[bass.ds(n, 1)].rearrange("o (t p) e -> p (o t) e", p=P),
                             fin[b].rearrange("p (t e) -> p t e", t=TT)).then_inc(f_out[b], 16)

            def ffn(n, b, m):
                if not isinstance(n, int) or n > 0:
                    store(n - 1, 1 - b)
                if not isinstance(n, int) or n + 3 < B:
                    load_expert(n + 3, 1 - b)

            slots(sp, slot, router)

            for u in (UNITS - 1, UNITS):
                last_slot(slot, u)
            load_expert(2, 0)
            ffn(0, 0, 0)
            router(1, 0)
            for n in range(1, 4):
                ffn(n, n % 2, n // 2)
            router(1, 5)
            ffn(4, 0, 2)
            with sp.Fori(2, (B - 4) // 2) as it:
                for i in (1, 2):
                    ffn(it * 2 + i, i % 2, it + i // 2)
            for n in (B - 3, B - 2):
                ffn(n, n % 2, n // 2)
            store(B - 2, 0)
            store(B - 1, 1)
            for b in range(2):
                sp.wait_ge(f_out[b], 16 * (B // 2))

        @block.scalar
        def _(act):
            def need_act(s, v):
                need(act, s, v)
                act.sem_inc(act_turn, 1)

            dt3, gt3 = ([m[l].rearrange("p (k n) -> p k n", k=3) for l in range(3)] for m in (DT, GT))

            def tile_gates(t):
                need(act, s_prod, t + 1)
                nc.scalar.activation(PT[:, 1, 0:LW[0]], PT[:, 1, 0:LW[0]], ACT.Copy, scale=0.5,
                                     accum_out=part[:, 2:3]).then_inc(s_psum, 1)

            def tile_synthesis(t):
                need(act, s_z, t + 1)
                nc.scalar.activation(ez, z, ACT.Exp).then_inc(s_ez, 1)
                need(act, s_wg, t + 1)
                if not first_tile(t):
                    need(act, s_recd, t)
                    need(act, s_shi, t * 2)
                nc.scalar.activation(GA[2], AA[2], ACT.Copy, scale=wg[:, 9:10]).then_inc(s_gate, 1)
                for l, kinds in ((2, (0, 1, 2)), (1, (0, 1, 2)), (0, (1, 2, 0))):
                    for c in kinds:
                        nc.scalar.activation(gt3[l][:, c, :], dt3[l][:, c, :], ACT.Copy,
                                             scale=wg[:, 3 * l + c:3 * l + c + 1]).then_inc(s_gate, 1)
                if not last_tile(t):
                    rows_out(act, need_act, t)

            def slot(u, n, k, lap):
                w, odd = u + 4, k % 2
                if unit_ok(u):
                    exponential(u, 0)
                if unit_ok(w):
                    need(act, s_d, w + 1)
                    need(act, s_lo, w - 1)
                    for o in range(2):
                        nc.scalar.activation(QF[:, odd, o, :], PM[:, o * S:(o + 1) * S], ACT.Identity,
                                             bias=bqk_sb[:, odd, o:o + 1]).then_inc(s_qa, 1)
                if unit_ok(u):
                    exponential(u, 1)
                if unit_ok(u + 1):
                    need_act(s_ms, u + 2)
                    for s in range(2):
                        act.dma_start(QP[KQ + s:KQ + s + 1, (k + 1) % RING, :, :].rearrange(
                            "p h (t q) -> p (h t) q", t=TT), mB[:, (k + 1) % 2, s, :]).then_inc(s_mrow, 16)
                if unit_ok(w):
                    need(act, s_r1, w + 1)
                    need(act, s_scr, (w - 1) * 16)
                    nc.scalar.copy(QB[:, odd, :, 1, :], QR[:, odd, :, :]).then_inc(s_mid, 1)
                if isinstance(u, int) and u == UNITS - 1:
                    act.wait_ge(s_p2, UNITS * 2)
                    split_1(1, 1, 0)
                    ffn_gelu(0, 0)
                if unit_ok(u):
                    need(act, s_pv, u * 2 + 2)
                    need(act, s_oc[k % 2], n * 32)
                    nc.scalar.copy(OS[:, k % 2, :, :].rearrange("p g t -> p (g t)"), PO[:, :]).then_inc(s_os, 1)
                if odd and image_ok(n + 3):
                    need(act, s_tr, n + 4)
                    need(act, s_v, n + 2)
                    need(act, s_d, u + 3)
                    nc.scalar.copy(xTH[:, (k // 2 + 3) % 2, :, :].rearrange("p c t -> p (c t)"),
                                   PM[:, :]).then_inc(s_xh, 1)

            def exponential(u, g):
                need(act, s_p2, u * 2 + (g + 1))
                need(act, s_pv, u * 2 + (g - 1))
                nc.scalar.activation(PT[:, g, :], S2[:, :], ACT.Exp, scale=float(D) ** -0.5).then_inc(s_exp, 1)

            def split_w1(t):
                nc.scalar.copy(w1H[:, :, :, :], w1_sb).then_inc(s_w1, 1)

            tiles(act, tile_gates, tile_synthesis, slot, split_w1)
            def router(part_, step):
                if step == 3:
                    need(act, f_ga, part_ + 1)
                    nc.scalar.activation(gact[:, 0:NR], PM[:, 0:NR], ACT.Gelu, bias=bp1_sb).then_inc(f_gae, 1)

            slots(act, slot, router)

            def ffn_xh(n, b):
                need(act, f_tr, n + 1)
                need(act, f_u, (n - 1) * 2)
                nc.scalar.copy(xH[b], PM[:, :]).then_inc(f_xh, 1)

            def split_1(n, b, m):
                act.wait_ge(f_wx1[b], (m + 1) * 16)
                need(act, f_u, (n - 1) * 2)
                nc.scalar.copy(wH[b][:, W1_], WX[b][:, W1_]).then_inc(f_h1, 1)

            def split_2(n, b, m):
                act.wait_ge(f_wx2[b], (m + 1) * 16)
                need(act, f_d, n - 1)
                nc.scalar.copy(wH[b][:, W2_], WX[b][:, W2_]).then_inc(f_h2, 1)

            def biases(n, b, m):
                act.wait_ge(f_wx2[b], (m + 1) * 16)
                need(act, f_r, (n - 1) * CH)
                nc.scalar.copy(WB[b], WX[b][:, CH * FF + FT * E:WX_W]).then_inc(f_wb, 1)

            def ffn_rh(n, b):
                need(act, f_d, n + 1)
                need(act, f_y, n - 1)
                for c in range(CH):
                    nc.scalar.activation(rH[b][:, c * S:(c + 1) * S], PO[:, c * S:(c + 1) * S], ACT.Identity,
                                         bias=WB[b][:, FT + c:FT + c + 1]).then_inc(f_rh, 1)

            def ffn_gelu(n, b):
                for j in range(2):
                    need(act, f_u, n * 2 + (j + 1))
                    need(act, f_wb, n + 1)
                    need(act, f_g, (n - 1) * 2)
                    for c in range(2):
                        f = 2 * j + c
                        src = (S1 if b == 0 else S2)[:, f * S:(f + 1) * S]
                        ins = nc.scalar.activation(gT[b][:, f * S:(f + 1) * S], src, ACT.Gelu, bias=WB[b][:, f:f + 1])
                        ins.then_inc(f_ge, 1)
                    half_ = slice(2 * j * S, 2 * (j + 1) * S)
                    need(act, f_d, n - 1)
                    need(act, f_ge, n * 4 + 2 * (j + 1))
                    nc.scalar.copy(gH[b][:, half_], gT[b][:, half_]).then_inc(f_gh, 1)

            def ffn(n, b, m):
                ffn_xh(n + 1, 1 - b)
                split_2(n + 1, 1 - b, m + b)
                ffn_rh(n, b)
                if not isinstance(n, int) or n + 2 < B:
                    split_1(n + 2, b, m + 1)
                ffn_gelu(n + 1, 1 - b)
                if not isinstance(n, int) or n + 2 < B:
                    biases(n + 2, b, m + 1)

            split_1(0, 0, 0)
            split_2(0, 0, 0)
            biases(0, 0, 0)
            act.wait_ge(s_d, UNITS)
            act.wait_ge(s_v, B)
            ffn_xh(0, 0)
            last_slot(slot, UNITS - 1)
            biases(1, 1, 0)
            for n in range(3):
                ffn(n, n % 2, n // 2)
            router(1, 3)
            ffn(3, 1, 1)
            images(act, ffn, B - 1, done=4)
            ffn_rh(B - 1, 1)

        @block.vector
        def _(dve):
            tt_ = dve.tensor_tensor

            def analysis(l):
                r, c = LVL[l]
                s, lo, hi = (m.rearrange("p (r c) -> p r c", r=2 * r) for m in (AA[l - 1], ALO[l], AHI[l]))
                d = DT[l].rearrange("p (k r c) -> p k r c", k=3, r=r)
                a = AA[l].rearrange("p (r c) -> p r c", r=r)
                tt_(lo, s[:, :, 0::2], s[:, :, 1::2], ALU.add)
                tt_(hi, s[:, :, 0::2], s[:, :, 1::2], ALU.subtract)
                dve.drain()
                tt_(a, lo[:, 0::2, :], lo[:, 1::2, :], ALU.add)
                tt_(d[:, 0], lo[:, 0::2, :], lo[:, 1::2, :], ALU.subtract)
                tt_(d[:, 1], hi[:, 0::2, :], hi[:, 1::2, :], ALU.add)
                tt_(d[:, 2], hi[:, 0::2, :], hi[:, 1::2, :], ALU.subtract)
                dve.drain()

            def synthesis(l):
                r, c = LVL[l]
                s, lo, hi = (m.rearrange("p (r c) -> p r c", r=2 * r) for m in (GA[l - 1], SLO[l], SHI[l]))
                d = GT[l].rearrange("p (k r c) -> p k r c", k=3, r=r)
                a = GA[l].rearrange("p (r c) -> p r c", r=r)
                tt_(lo[:, 0::2, :], a, d[:, 0], ALU.add)
                tt_(lo[:, 1::2, :], a, d[:, 0], ALU.subtract)
                tt_(hi[:, 0::2, :], d[:, 1], d[:, 2], ALU.add)
                tt_(hi[:, 1::2, :], d[:, 1], d[:, 2], ALU.subtract)
                dve.drain()
                tt_(s[:, :, 0::2], lo, hi, ALU.add)
                tt_(s[:, :, 1::2], lo, hi, ALU.subtract)
                dve.drain()

            def low_columns(t):
                need(dve, s_x, (t + 1) * 16)
                tt_(alo3, x3[:, :, 0::2], x3[:, :, 1::2], ALU.add).then_inc(s_xfree, 1)

            def low_details(t):
                dve.drain()
                if not first_tile(t):
                    need(dve, s_gate, t * 10)
                tt_(AA[0].rearrange("p (r c) -> p r c", r=fr), alo3[:, 0::2, :], alo3[:, 1::2, :], ALU.add)
                tt_(d4[:, 0], alo3[:, 0::2, :], alo3[:, 1::2, :], ALU.subtract)
                dve.drain()
                dve.sem_inc(s_part, 1)

            scrap = {(0, 0): PT[:, 0, :], (0, 1): S1[:, :]}
            for l, bank in ((1, S2[:, :]), (2, PO[:, :])):
                for j in range(3):
                    scrap[l, j] = bank[:, j * LW[l]:(j + 1) * LW[l]]

            def tile_gates(t):
                analysis(1)
                analysis(2)
                na = LVL[2][0] * LVL[2][1]
                if first_tile(t):
                    dve.wait_ge(s_wdc, 16 * IPT)
                if not first_tile(t):
                    need(dve, s_zps, t)
                dve.tensor_tensor_reduce(PO[:, 3 * LW[2]:3 * LW[2] + na], AA[2], WD[:, WD_OFF[3]:WD_OFF[3] + na], 0.125,
                                         0.0, ALU.mult, ALU.add, part[:, 9:10]).then_inc(s_part, 1)
                for l, j in ((2, 0), (2, 1), (2, 2), (1, 0), (1, 1), (1, 2), (0, 0), (0, 1)):
                    w0 = WD_OFF[l] + j * LW[l]
                    if l == 0:
                        if first_tile(t):
                            dve.wait_ge(s_wd, 16 * (IPT + 1))
                        need(dve, s_dhi, (t + 1) * 2)
                    ins = dve.tensor_tensor_reduce(scrap[l, j], DT[l], WD[:, w0:w0 + LW[l]], 0.5 ** (l + 1), 0.0,
                                                   ALU.mult, ALU.add, part[:, 3 * l + j:3 * l + j + 1])
                dve.drain()
                dve.sem_inc(s_part, 2)

            def tile_synthesis(t):
                need(dve, s_zps, t + 1)
                tt_(z, PM[:, 0:10], bdt, ALU.add)
                dve.drain()
                z3 = z[:, 0:9].rearrange("p (l c) -> p l c", l=3)
                dve.tensor_reduce(zmax, z3, AX, ALU.max)
                dve.tensor_scalar(z[:, 9:10], z[:, 9:10], -1.0, None, ALU.mult)
                dve.drain()
                tt_(z3, z3, zmax.rearrange("p (l o) -> p l o", o=1).to_broadcast([P, 3, 3]),
                    ALU.subtract).then_inc(s_z, 1)
                need(dve, s_ez, t + 1)
                dve.tensor_reduce(zsum[:, 0:3], ez[:, 0:9].rearrange("p (l c) -> p l c", l=3), AX, ALU.add)
                dve.tensor_scalar(zsum[:, 3:4], ez[:, 9:10], 1.0, None, ALU.add)
                tt_(es[:, 0:9], ez[:, 0:9], wscale[:, 0:9], ALU.mult)
                dve.drain()
                dve.reciprocal(zrec, zsum)
                dve.drain()
                tt_(wg[:, 0:9].rearrange("p (l c) -> p l c", l=3), es[:, 0:9].rearrange("p (l c) -> p l c", l=3),
                    zrec[:, 0:3].rearrange("p (l o) -> p l o", o=1).to_broadcast([P, 3, 3]), ALU.mult)
                tt_(wg[:, 9:10], zrec[:, 3:4], wscale[:, 9:10], ALU.mult)
                dve.drain()
                dve.sem_inc(s_wg, 1)
                if not last_tile(t):
                    low_columns(t + 1)
                need(dve, s_gate, t * 10 + 4)
                synthesis(2)
                need(dve, s_gate, t * 10 + 7)
                synthesis(1)
                need(dve, s_gate, t * 10 + 10)
                a = GA[0].rearrange("p (r c) -> p r c", r=fr)
                tt_(slo3[:, 0::2, :], a, g4[:, 0], ALU.add)
                tt_(slo3[:, 1::2, :], a, g4[:, 0], ALU.subtract)
                dve.drain()
                dve.sem_inc(s_slo, 1)
                if not last_tile(t):
                    low_details(t + 1)
                need(dve, s_shi, (t + 1) * 2)
                if not first_tile(t):
                    need(dve, s_h0, t * (16 * IPT * TT))
                columns_merged(dve, 0, VROWS).then_inc(s_recd, 1)

            low_columns(0)
            low_details(0)
            dve.wait_ge(s_cst, CONSTANTS)

            def ln_stat(n, b, done):
                for tt in range(TT):
                    dve.bn_stats(stat[:, b, tt, :], h_row(n, tt))
                dve.drain()
                for tt in range(TT):
                    dve.bn_aggr(mv[:, b, tt, :], stat[:, b, tt, :])
                dve.drain()
                dve.tensor_scalar(ve[:, b, :], mv[:, b, :, 1], EPS, None, ALU.add).then_inc(done, 1)

            def ln_apply(n, b, rs, free, freed, done):
                need(dve, rs, n + 1)
                need(dve, free, freed)
                for tt in range(TT):
                    dve.tensor_scalar(xn[:, b, tt, :], h_row(n, tt), mv[:, b, tt, 0:1], rstd[:, b, tt:tt + 1],
                                      ALU.subtract, ALU.mult).then_inc(done, 1)

            def slot(u, n, k, lap):
                v, w, odd = u + 2, u + 4, k % 2
                b3 = (k // 2 + 3) % 2
                if unit_ok(u - 2):
                    normalise(u, n, k)
                elif not odd and image_ok(n + 2):
                    low_part(u, n, k)
                if unit_ok(v):
                    row_max(v, k + 2, 0)
                if unit_ok(u + 1):
                    b = (k + 1) % 2
                    need(dve, s_mt, u + 2)
                    need(dve, s_mrow, u * 32)
                    dve.tensor_scalar(mB[:, b, 0, :], PM[0:TT * HU, 0:P], -1.0, None, ALU.mult)
                    dve.drain()
                    dve.scalar_tensor_tensor(out=mB[:, b, 1, :], in0=PM[0:TT * HU, 0:P], scalar=-1.0,
                                             in1=mB[:, b, 0, :], op0=ALU.mult, op1=ALU.subtract).then_inc(s_ms, 1)
                if unit_ok(w):
                    need(dve, s_qa, (w + 1) * 2)
                    need(dve, s_scr, (w - 1) * 16)
                    dve.tensor_copy(QB[:, odd, :, 0, :], QF[:, odd, :, :]).then_inc(s_hi, 1)
                if not odd and image_ok(n + 3):
                    dve.wait_ge(s_h0, 16 * TT * IPT * ((n + 3) // IPT + 1 if isinstance(n, int) else TILES))
                    ln_stat(n + 3, b3, s_stat)
                if odd and image_ok(n + 3):
                    ln_apply(n + 3, b3, s_rstd, s_tr, n + 2, s_xn)
                if unit_ok(v):
                    row_max(v, k + 2, 1)
                if not odd and image_ok(n + 1):
                    need(dve, s_v, n + 2)
                    need(dve, s_pv, n * 4)
                    tt_(Va[:, (k // 2 + 1) % 2, :, :, :, 0], PM[:, :].rearrange("p (t h d) -> p t h d", t=TT, h=H),
                        bv_sb[:, :].rearrange("p (o h d) -> p o h d", o=1, h=H).to_broadcast([P, TT, H, D]),
                        ALU.add).then_inc(s_va, 1)
                if isinstance(u, int) and u == UNITS - 1:
                    ffn_gl(0, 0)
                if odd and image_ok(n - 1):
                    join(n - 1)

            def normalise(u, n, k):
                need(dve, s_oc[k % 2], n * 32)
                dve.reciprocal(SC[:, k % 2, :], SC[:, k % 2, :])
                dve.drain()
                if k % 2 == 0 and image_ok(n + 2):
                    low_part(u, n, k)
                need(dve, s_wp, n - 1)
                tt_(AC[:, (k - 2) % RING, :], AU[:, k % 2, :], SC[:, k % 2, :], ALU.mult).then_inc(s_ac, 1)

            def low_part(u, n, k):
                need(dve, s_xh, n + 3)
                need(dve, s_v, n + 1)
                need(dve, s_d, u + 2)
                b = (k // 2 + 2) % 2
                tt_(xTL[:, b, :, :].rearrange("p c t -> p (c t)"), PM[:, :],
                    xTH[:, b, :, :].rearrange("p c t -> p (c t)"), ALU.subtract).then_inc(s_xt, 1)

            def join(n):
                need(dve, s_wp, n + 1)
                need(dve, s_bp, (n + 1) * TT)
                a = hN[:, bass.ds(n * TT, TT), :]
                tt_(a, a, PM[:, :].rearrange("p (t e) -> p t e", t=TT), ALU.add).then_inc(s_h2, 1)

            def row_max(v, kv, g):
                b = kv % 2
                need(dve, s_p1, v * 2 + (g + 1))
                need(dve, s_mt, v - 1)
                m = mx[:, b, :].rearrange("p (h t) -> p h t", t=TT)[:, GH * g:GH * (g + 1), :]
                dve.tensor_reduce(m[:, :, 1],
                                  S1[:, 0:1024].rearrange("p (h q) -> p h q", h=GH), AX, ALU.max).then_inc(s_mx, 1)
                dve.tensor_reduce(m[:, :, 0],
                                  S1[:, 1024:1536].rearrange("p (h q) -> p h q", h=GH), AX, ALU.max).then_inc(s_mx, 1)

            tiles(dve, tile_gates, tile_synthesis, slot)

            def router(part_, step):
                lr = lastr[0:NR, :]
                if step == 1:
                    dve.wait_ge(f_last, 16 * (part_ + 1))
                    if part_ == 0:
                        dve.wait_ge(f_w, 16 * 6)
                        dve.tensor_scalar(bo3, bo3, 0.3, None, ALU.mult)
                    dve.bn_stats(lstat[0:NR, :], lr)
                    dve.drain()
                    dve.bn_aggr(lmv[0:NR, :], lstat[0:NR, :])
                    dve.drain()
                    dve.tensor_scalar(lve[0:NR, :], lmv[0:NR, 1:2], EPS, None, ALU.add).then_inc(f_lst, 1)
                    dve.wait_ge(f_lrs, part_ + 1)
                    dve.tensor_scalar(lr, lr, lmv[0:NR, 0:1], lrstd[0:NR, :], ALU.subtract, ALU.mult).then_inc(f_ln, 1)
                if step == 2:
                    dve.wait_ge(f_lt, part_ + 1)
                    dve.tensor_copy(lastT[:, 0:CH * NR], PM[:, 0:CH * NR]).then_inc(f_lte, 1)
                if step == 4:
                    dve.wait_ge(f_lg, part_ + 1)
                    tt_(logit[0:NR, :], PM[0:NR, 0:NX], bp2_sb[0:NR, :], ALU.add).then_inc(f_lge, 1)
                    dve.drain()
                    dve.max(top8[0:NR, :], logit[0:NR, :])
                    dve.drain()
                    dve.max_index(idx8[:, part_, :], top8[0:NR, :], logit[0:NR, :]).then_inc(f_idx, 1)
                    dve.drain()

            def ffn_in(n, b):
                ln_stat(n, b, f_stat)
                need(dve, f_base, (n - 1) * TT)
                ln_apply(n, b, f_rstd, f_tr, n - 1, f_xn)

            def ffn_xt(n, b):
                need(dve, f_xh, n + 1)
                need(dve, f_u, (n - 1) * 2)
                tt_(xL[b], PM[:, :], xH[b], ALU.subtract).then_inc(f_xt, 1)

            def ffn_gl(n, b):
                need(dve, f_d, n - 1)
                for j in range(2):
                    half_ = slice(2 * j * S, 2 * (j + 1) * S)
                    need(dve, f_gh, n * 2 + (j + 1))
                    tt_(gL[b][:, half_], gT[b][:, half_], gH[b][:, half_], ALU.subtract).then_inc(f_g, 1)

            def ffn_rl(n, b):
                need(dve, f_rh, (n + 1) * CH)
                need(dve, f_y, n - 1)
                for c in range(CH):
                    dve.scalar_tensor_tensor(out=rL[b][:, c * S:(c + 1) * S], in0=PO[:, c * S:(c + 1) * S],
                                             scalar=WB[b][:, FT + c:FT + c + 1], in1=rH[b][:, c * S:(c + 1) * S],
                                             op0=ALU.add, op1=ALU.subtract).then_inc(f_r, 1)

            def ffn_base(n, b, m):
                need(dve, f_base, (n + 1) * TT)
                need(dve, f_out[b], m * 16)
                for tt in range(TT):
                    tt_(fin[b][:, tt * E:(tt + 1) * E], h_row(n, tt), bo3, ALU.add)
                dve.drain()

            def ffn_fin(n, b):
                need(dve, f_y, n + 1)
                for tt in range(TT):
                    f = fin[b][:, tt * E:(tt + 1) * E]
                    dve.scalar_tensor_tensor(out=f, in0=y_ps(b)[:, tt * E:(tt + 1) * E], scalar=0.3, in1=f,
                                             op0=ALU.mult, op1=ALU.add).then_inc(f_fin, 1)

            def ffn(n, b, m):
                ffn_xt(n + 1, 1 - b)
                if not isinstance(n, int) or n + 2 < B:
                    ffn_in(n + 2, b)
                ffn_rl(n, b)
                ffn_base(n, b, m)
                ffn_gl(n + 1, 1 - b)
                ffn_fin(n, b)

            slots(dve, slot, router)
            ffn_in(0, 0)
            dve.wait_ge(s_d, UNITS)
            dve.wait_ge(s_v, B)
            ffn_xt(0, 0)
            ffn_in(1, 1)
            dve.tensor_copy(woH, wo_sb)
            dve.drain()
            tt_(woL, wo_sb, woH, ALU.subtract).then_inc(f_wo, 1)
            last_slot(slot, UNITS - 1)
            last_slot(slot, UNITS)
            ffn_xt(1, 1)
            ffn_in(2, 0)
            normalise(UNITS + 1, B, UNITS + 1)
            ffn_rl(0, 0)
            ffn_base(0, 0, 0)
            ffn_gl(1, 1)
            ffn_fin(0, 0)
            join(B - 1)
            ffn_xt(2, 0)
            ffn_in(3, 1)
            router(1, 1)
            ffn_rl(1, 1)
            ffn_base(1, 1, 0)
            ffn_gl(2, 0)
            ffn_fin(1, 1)
            router(1, 2)
            for n in range(2, 4):
                ffn(n, n % 2, n // 2)
            router(1, 4)
            images(dve, ffn, B - 1, done=4)
            ffn_rl(B - 1, 1)
            ffn_base(B - 1, 1, B // 2 - 1)
            ffn_fin(B - 1, 1)

        @block.tensor
        def _(pe):
            mm = pe.matmul

            def three(out_, w_parts, x_parts, pick_w, pick_x, start, stop):
                (wh, wl), (xh, xl) = w_parts, x_parts
                mm(out_, pick_w(wh), pick_x(xh), start=start, stop=False)
                mm(out_, pick_w(wh), pick_x(xl), start=False, stop=False)
                return mm(out_, pick_w(wl), pick_x(xh), start=False, stop=stop)

            pe.wait_ge(s_cst, CONSTANTS)
            def tile(t):
                if last_tile(t):
                    pe.wait_ge(s_qa, 2)
                need(pe, s_part, (t + 1) * 4)
                need(pe, s_psum, t + 1)
                mm(PM[:, 0:10], blkones[:, :], part, start=True, stop=True).then_inc(s_zps, 1)

            def scores_max(v, kv, lap, g):
                r = kv % RING
                if g == 0:
                    need(pe, s_qp[r], (lap + kv // RING + 1) * 96)
                need(pe, s_mx, v * 4 + 2 * g)
                for hh in range(0, GH, 2):
                    dst = S1[:, hh * S:(hh + 2) * S].rearrange("p (h q) -> p h q", h=2)[:, :, P:S]
                    mm(dst, identb[:, :], maskb[:, :].rearrange("p (o k) -> p o k", o=1).to_broadcast([P, 2, P]),
                       start=True, stop=False, skip_group_check=True)
                mm(S1[:, 1024:1536].rearrange("p (h q) -> p h q", h=GH), identb[:, :],
                   maskb[:, :].rearrange("p (o k) -> p o k", o=1).to_broadcast([P, GH, P]),
                   start=True, stop=False, skip_group_check=True)
                for j in range(GH):
                    h = GH * g + j
                    mm(S1[:, j * S:(j + 1) * S], QP[0:KQ, r, h, P:S], KP[0:KQ, r, h, :],
                       start=False, stop=True, skip_group_check=True)
                for j in range(GH):
                    h = GH * g + j
                    ins = mm(S1[:, 1024 + j * P:1024 + (j + 1) * P], QP[0:KQ, r, h, 0:P], KP[0:KQ, r, h, 0:P],
                             start=False, stop=True, skip_group_check=True)
                ins.then_inc(s_p1, 1)

            def scores_exp(u, k, g):
                if g == 0:
                    need(pe, s_mrow, (u + 1) * 32)
                need(pe, s_exp, u * 2 + g)
                for j in range(GH):
                    h = GH * g + j
                    mm(S2[:, j * S:(j + 1) * S], KP[0:KM, k % RING, h, 0:P], QP[0:KM, k % RING, h, :],
                       start=True, stop=True)
                for j in range(GH):
                    h = GH * g + j
                    ins = mm(S2[:, 1024 + j * P:1024 + (j + 1) * P], KP[0:KM, k % RING, h, P:S],
                             QP[0:KM, k % RING, h, P:S], start=True, stop=True)
                ins.then_inc(s_p2, 1)

            def weighted(u, n, k, g):
                if g == 0:
                    need(pe, s_os, u)
                    need(pe, s_va, n + 1)
                need(pe, s_sel, u * 4 + 2 * (g + 1))
                vb = Va[:, (k // 2) % 2, :, :, :, :]
                for kt in range(TT):
                    for j in range(GH):
                        h = (k % 2) * HU + GH * g + j
                        if kt == 0:
                            dst, pr = PO[32 * j:32 * j + 32, g * S:(g + 1) * S], PT[:, g, j * S:(j + 1) * S]
                        else:
                            dst = PO[32 * j:32 * j + 32, g * S + P:(g + 1) * S]
                            pr = PT[:, g, 1024 + j * P:1024 + (j + 1) * P]
                        ins = mm(dst, vb[:, kt, h, :, :].rearrange("p d c -> p (d c)"), pr,
                                 start=(kt == 0), stop=(kt == 1), skip_group_check=True)
                ins.then_inc(s_pv, 1)

            def pm_free(u, n, odd, step, sem_, count):
                if not isinstance(u, int):
                    return need(pe, sem_, count)
                if u >= UNITS - 1:
                    need(pe, f_xt, 1 if u < UNITS else 2)
                if u > ROUTE0 + 2:
                    need(pe, (f_lte, f_gae, f_lge)[min(u - ROUTE0 - 3, 2)], 1)
                if u < 0:
                    need(pe, s_z, TILES if u > FIRST + 2 else TILES - 1)
                need(pe, s_qa, 2 * min(u + 4 + (step > 0), UNITS))
                need(pe, s_ms, min(u + 1 + (step > 1), UNITS))
                need(pe, s_va, min(n + 1 + (odd or step > 2), B))
                need(pe, s_h2, min(n - 1 + (odd and step > 2), B))
                need(pe, s_xt, min(n + 3, B))

            def slot(u, n, k, lap):
                v, w, odd = u + 2, u + 4, k % 2
                if unit_ok(u):
                    scores_exp(u, k, 0)
                if unit_ok(v):
                    scores_max(v, k + 2, lap, 0)
                if isinstance(w, int) and w == 0:
                    pe.wait_ge(s_w1, 2)
                if unit_ok(w):
                    if odd:
                        pm_free(u, n, odd, 0, s_va, n + 2)
                    else:
                        pm_free(u, n, odd, 0, s_xt, n + 3)
                    for o in range(2):
                        for c in range(CH):
                            ins = three(PM[:, o * S:(o + 1) * S], (w1H, w1L), (xTH, xTL),
                                        lambda w_: w_[:, c, o, odd * P:(odd + 1) * P],
                                        lambda x_: x_[:, (k // 2) % 2, c, :], start=(c == 0), stop=(c == CH - 1))
                    ins.then_inc(s_d, 1)
                if unit_ok(u):
                    scores_exp(u, k, 1)
                if isinstance(u, int) and u == UNITS - 1:
                    pe.wait_ge(s_mx, UNITS * 4)
                    ffn_up(0, 0, 0)
                if unit_ok(u + 1):
                    pm_free(u, n, odd, 1, s_qa, (u + 5) * 2)
                    need(pe, s_mx, (u + 2) * 4)
                    pe.transpose(PM[0:TT * HU, 0:P], mx[:, (k + 1) % 2, :], ident[:, :]).then_inc(s_mt, 1)
                if unit_ok(u):
                    weighted(u, n, k, 0)
                if unit_ok(v):
                    scores_max(v, k + 2, lap, 1)
                if not odd and image_ok(n + 1):
                    pm_free(u, n, odd, 2, s_ms, u + 2)
                    for tt in range(TT):
                        for c in range(CH):
                            ins = three(PM[:, tt * E:(tt + 1) * E], (xTH, xTL), (w1H, w1L),
                                        lambda x_: x_[:, (k // 2 + 1) % 2, c, tt * P:(tt + 1) * P],
                                        lambda w_: w_[:, c, 2, :], start=(c == 0), stop=(c == CH - 1))
                    ins.then_inc(s_v, 1)
                if odd and image_ok(n - 1):
                    pm_free(u, n, odd, 2, s_ms, u + 2)
                    need(pe, s_ac, n * 2)
                    for tt in range(TT):
                        for c in range(UPI):
                            ins = mm(PM[:, tt * E:(tt + 1) * E],
                                     AC[:, ((k // 2 - 1) * 2 + c) % RING, tt * P:(tt + 1) * P],
                                     wp_sb[:, c, :], start=(c == 0), stop=(c == UPI - 1))
                    ins.then_inc(s_wp, 1)
                if unit_ok(u):
                    weighted(u, n, k, 1)
                if odd and image_ok(n + 3):
                    pm_free(u, n, odd, 3, s_h2, n)
                    need(pe, s_xn, (n + 4) * TT)
                    for c in range(CH):
                        for tt in range(TT):
                            ins = pe.transpose(PM[:, c * S + tt * P:c * S + (tt + 1) * P],
                                               xn[:, (k // 2 + 3) % 2, tt, c * P:(c + 1) * P], ident[:, :])
                    ins.then_inc(s_tr, 1)

            tiles(pe, nothing, tile, slot)

            def router(part_, step):
                if step == 2:
                    pe.wait_ge(f_ln, part_ + 1)
                    settle(part_, step)
                    for c in range(CH):
                        ins = pe.transpose(PM[:, c * NR:(c + 1) * NR], lastr[0:NR, c * P:(c + 1) * P], ident[0:NR, 0:NR])
                    ins.then_inc(f_lt, 1)
                if step == 3:
                    settle(part_, step)
                    pe.wait_ge(f_lte, part_ + 1)
                    for c in range(CH):
                        ins = mm(PM[:, 0:NR], wp1_sb[:, c * NAV:(c + 1) * NAV], lastT[:, c * NR:(c + 1) * NR],
                                 start=(c == 0), stop=(c == CH - 1))
                    ins.then_inc(f_ga, 1)
                if step == 4:
                    settle(part_, step)
                    pe.wait_ge(f_gae, part_ + 1)
                    mm(PM[0:NR, 0:NX], gact[:, 0:NR], wp2_sb, start=True, stop=True).then_inc(f_lg, 1)

            def settle(part_, step):
                if part_ == 0:
                    u = ROUTE0 + step
                    need(pe, s_qa, 2 * min(u + 5, UNITS))
                    need(pe, s_ms, min(u + 2, UNITS))
                    need(pe, s_va, min(u // 2 + 2, B))
                    need(pe, s_h2, min((u - 1) // 2, B))
                else:
                    pe.wait_ge(f_xt, step + 1)

            def ffn_tr(n, b):
                need(pe, f_xn, (n + 1) * TT)
                need(pe, f_xt, n)
                for c in range(CH):
                    for tt in range(TT):
                        ins = pe.transpose(PM[:, c * S + tt * P:c * S + (tt + 1) * P], xn[:, b, tt, c * P:(c + 1) * P],
                                           ident[:, :])
                ins.then_inc(f_tr, 1)

            def ffn_up(n, b, m):
                need(pe, f_xt, n + 1)
                need(pe, f_l1, n + 1)
                need(pe, f_ge, (n - 1) * FT)
                for f in range(FT):
                    for c in range(CH):
                        w0 = c * FF + f * P
                        ins = three((S1 if b == 0 else S2)[:, f * S:(f + 1) * S], (wH[b], wL[b]), (xH[b], xL[b]),
                                    lambda w: w[:, w0:w0 + P], lambda x_: x_[:, c * S:(c + 1) * S],
                                    start=(c == 0), stop=(c == CH - 1))
                    if f % 2:
                        ins.then_inc(f_u, 1)

            def ffn_down(n, b):
                need(pe, f_l2, n + 1)
                need(pe, f_r, n * CH)
                for c in range(CH):
                    for f in range(FT):
                        if c == 0 and f % 2 == 0:
                            need(pe, f_g, n * 2 + (f // 2 + 1))
                        w0 = CH * FF + f * E + c * P
                        ins = three(PO[:, c * S:(c + 1) * S], (wH[b], wL[b]), (gH[b], gL[b]),
                                    lambda w: w[:, w0:w0 + P], lambda g_: g_[:, f * S:(f + 1) * S],
                                    start=(f == 0), stop=(f == FT - 1))
                ins.then_inc(f_d, 1)

            def ffn_y(n, b):
                need(pe, f_r, (n + 1) * CH)
                need(pe, f_fin, (n - 1) * TT)
                for tt in range(TT):
                    for c in range(CH):
                        t0 = c * S + tt * P
                        ins = three(y_ps(b)[:, tt * E:(tt + 1) * E], (rH[b], rL[b]), (woH, woL),
                                    lambda r_: r_[:, t0:t0 + P], lambda w: w[:, c * E:(c + 1) * E],
                                    start=(c == 0), stop=(c == CH - 1))
                ins.then_inc(f_y, 1)

            def ffn(n, b, m):
                ffn_tr(n + 1, 1 - b)
                ffn_down(n, b)
                ffn_up(n + 1, 1 - b, m + b)
                ffn_y(n, b)

            slots(pe, slot, router)
            pe.wait_ge(s_ms, UNITS)
            ffn_tr(0, 0)
            last_slot(slot, UNITS - 1)
            pe.wait_ge(s_h2, B - 1)
            pe.wait_ge(s_os, UNITS)
            pe.wait_ge(s_exp, UNITS * 2)
            pe.wait_ge(f_wo, 1)
            ffn(0, 0, 0)
            last_slot(slot, UNITS + 1)
            pe.wait_ge(s_h2, B)
            ffn(1, 1, 0)
            for step, out_of_pm in ((2, f_lte), (3, f_gae)):
                router(1, step)
                pe.wait_ge(out_of_pm, 2)
                ffn(step, step % 2, 1)
            router(1, 4)
            pe.wait_ge(f_lge, 2)
            images(pe, ffn, B - 1, done=4)
            ffn_down(B - 1, 1)
            ffn_y(B - 1, 1)


def layouts(a):
    c = np.ascontiguousarray
    img = a["x"].reshape(TILES, P, 8 * E)
    fine = []
    for name, (r, w) in zip(("L0_tok_Wd3", "L0_tok_Wd2", "L0_tok_Wd1"), LVL):
        fine.append(a[name].reshape(3, BLK, r, w, 3).transpose(1, 4, 0, 2, 3).reshape(BLK, -1))
    wd = np.concatenate(fine + [a["L0_tok_Wa"].reshape(BLK, -1)], axis=1)
    bd = np.concatenate([a["L0_tok_bd3"], a["L0_tok_bd2"], a["L0_tok_bd1"], a["L0_tok_ba"]]).reshape(1, 10)
    w1 = a["L0_attn_W1"].reshape(CH, P, H, 3, D)
    qk = w1[:, :, :, 0:2].reshape(CH, P, UPI, HU, 2, D).transpose(1, 0, 4, 2, 5, 3).reshape(P, CH, 2, E)
    v = w1[:, :, :, 2].transpose(1, 0, 2, 3).reshape(P, CH, 1, E)
    b1 = a["L0_attn_b1"].reshape(H, 3, D)
    bqk = b1[:, 0:2].reshape(UPI, HU, 2, D).transpose(3, 1, 0, 2).reshape(P, UPI, 2)
    wp = a["L0_attn_Wp"].reshape(UPI, 2, GH, D, E).transpose(2, 3, 1, 0, 4).reshape(P, UPI, E)
    wx = np.concatenate([
        a["L0_ffn_W1"].reshape(NX, CH, P, FF).transpose(0, 2, 1, 3).reshape(NX, P, -1),
        a["L0_ffn_W2"].reshape(NX, FT, P, E).transpose(0, 2, 1, 3).reshape(NX, P, -1),
        a["L0_ffn_b1"].reshape(NX, FT, P).transpose(0, 2, 1),
        a["L0_ffn_b2"].reshape(NX, CH, P).transpose(0, 2, 1)], axis=2)
    rows = lambda m: m.reshape(-1, P, m.shape[1]).transpose(1, 0, 2).reshape(P, -1)
    return {
        "x": c(img), "wd": c(wd), "bd": c(bd), "w1": c(np.concatenate([qk, v], axis=2)), "bqk": c(bqk),
        "bv": c(b1[:, 2].reshape(1, E)), "wp": c(wp), "bp": c(a["L0_attn_bp"].reshape(1, E)),
        "wp1": c(rows(a["L0_ffn_Wp1"])), "bp1": c(a["L0_ffn_bp1"].reshape(P, 1)), "wp2": c(a["L0_ffn_Wp2"]),
        "bp2": c(a["L0_ffn_bp2"].reshape(1, NX)), "wx": c(wx), "wo": c(rows(a["L0_ffn_Wo"])),
        "bo": c(a["L0_ffn_bo"].reshape(1, E)),
    }


def kernel(**inputs):
    import concourse.bacc as bacc
    from concourse.bass_utils import run_bass_kernel_spmd

    nc = bacc.Bacc("TRN2", target_bir_lowering=False, num_devices=1)
    arrays = layouts({k: np.asarray(v) for k, v in inputs.items()})
    args = {k: nc.dram_tensor(f"in_{k}", v.shape, mybir.dt.from_np(v.dtype), kind="ExternalInput").ap()
            for k, v in arrays.items()}
    args["out"] = nc.dram_tensor("out_h", (B, S, E), F32, kind="ExternalOutput").ap()
    tower(nc, **args)
    r = run_bass_kernel_spmd(nc, [{f"in_{k}": v for k, v in arrays.items()}], core_ids=[0])
    return r.results[0]["out_h"]
```
